# Optimizing a Trainium2 kernel written in Bass

```python
import numpy as np
import jax
import jax.numpy as jnp

def _softmax(x, axis=-1):
    return jax.nn.softmax(x, axis=axis)

def _gelu(x):
    return jax.nn.gelu(x, approximate=True)

def _silu(x):
    return jax.nn.silu(x)

def _sigmoid(x):
    return jax.nn.sigmoid(x)

def _layernorm(x, axis=-1, eps=1e-05):
    m = jnp.mean(x, axis=axis, keepdims=True)
    v = jnp.var(x, axis=axis, keepdims=True)
    return (x - m) / jnp.sqrt(v + eps)

def _scatter_add(tgt, idx, src, axis=0):
    return tgt.at[idx].add(src)

def _segment_sum(src, seg, n):
    return jax.ops.segment_sum(src, seg, n)
kernel_name = 'mk_gnn_ffn_d1_gnn_r32_e03890'

def setup_inputs(seed: int=0):
    np.random.seed(seed)
    _w = jnp.asarray

    def _rec_inputs():
        import jax
        import jax.numpy as jnp
        _gk = jax.random.key(seed)
        x = -8.776e-05 + 1 * jax.random.normal(jax.random.fold_in(_gk, 1), (10000, 512), jnp.float32)
        _s = jax.random.randint(jax.random.fold_in(_gk, 2), (5000,), 0, 10000, jnp.int32)
        _d = jax.random.randint(jax.random.fold_in(_gk, 3), (5000,), 0, 10000, jnp.int32)
        _loop = jnp.arange(10000, dtype=jnp.int32)
        src = jnp.concatenate([_s, _d, _loop])
        dst = jnp.concatenate([_d, _s, _loop])
        _o = jnp.argsort(dst, stable=True)
        src = src[_o]
        dst = dst[_o]
        return (x, src, dst)
    x, src, dst = _rec_inputs()

    def _L0_gnn_setup():
        import jax, jax.numpy as jnp
        import numpy as np
        N_NODES = 10000
        N_EDGES = 5000
        IN_DIM = 512
        HID = 256
        HEADS = 4
        OUT_DIM = 512
        NEG_SLOPE = 0.2

        def _glorot(key, shape):
            fan_in, fan_out = (shape[0], shape[-1])
            lim = jnp.sqrt(6.0 / (fan_in + fan_out))
            return jax.random.uniform(key, shape, jnp.float32, -lim, lim)

        def gat_conv(x, src, dst, W, att_src, att_dst, bias):
            N = x.shape[0]
            h = (x @ W).reshape(N, HEADS, HID)
            a_src = jnp.sum(h * att_src, axis=-1)
            a_dst = jnp.sum(h * att_dst, axis=-1)
            e = jax.nn.leaky_relu(a_src[src] + a_dst[dst], NEG_SLOPE)
            m = jax.ops.segment_max(e, dst, num_segments=N)
            e = jnp.exp(e - m[dst])
            s = jax.ops.segment_sum(e, dst, num_segments=N)
            alpha = e / (s[dst] + 1e-16)
            msg = alpha[:, :, None] * h[src]
            out = jax.ops.segment_sum(msg, dst, num_segments=N)
            return out.reshape(N, HEADS * HID) + bias
        key = jax.random.key(seed)
        ks = jax.random.split(key, 16)
        x = jax.random.normal(ks[0], (N_NODES, IN_DIM), jnp.float32)
        edge_index = jax.random.randint(ks[1], (2, N_EDGES), 0, N_NODES, jnp.int64)
        W1 = _glorot(ks[2], (IN_DIM, HEADS * HID))
        att_src1 = _glorot(ks[3], (HEADS, HID))
        att_dst1 = _glorot(ks[4], (HEADS, HID))
        b1 = jnp.zeros((HEADS * HID,), jnp.float32)
        W2 = _glorot(ks[5], (HEADS * HID, HEADS * HID))
        att_src2 = _glorot(ks[6], (HEADS, HID))
        att_dst2 = _glorot(ks[7], (HEADS, HID))
        b2 = jnp.zeros((HEADS * HID,), jnp.float32)
        fcW = _glorot(ks[8], (HEADS * HID, OUT_DIM))
        fcb = jnp.zeros((OUT_DIM,), jnp.float32)
        return dict(x=x, edge_index=edge_index, W1=W1, att_src1=att_src1, att_dst1=att_dst1, b1=b1, W2=W2, att_src2=att_src2, att_dst2=att_dst2, b2=b2, fcW=fcW, fcb=fcb)
    _L0_gnn_all = _L0_gnn_setup()
    _L0_gnn_in = {k: v for k, v in _L0_gnn_all.items() if k in ('W1', 'att_src1', 'att_dst1', 'b1', 'W2', 'att_src2', 'att_dst2', 'b2', 'fcW', 'fcb')}
    del _L0_gnn_all

    def _L0_ffn_setup():
        import jax, jax.numpy as jnp
        import numpy as np
        SINKHORN_ITERS = 8
        TEMPERATURE = 1.0
        EPS = 1e-10

        def sinkhorn(gates):
            t = jnp.log(jnp.clip(gates, EPS)) / TEMPERATURE

            def body(t, _):
                t = t - jax.nn.logsumexp(t, axis=-2, keepdims=True)
                t = t - jax.nn.logsumexp(t, axis=-1, keepdims=True)
                return (t, None)
            t, _ = jax.lax.scan(body, t, None, length=SINKHORN_ITERS)
            return jnp.exp(t)
        key = jax.random.key(seed)
        k1, k2, k3 = jax.random.split(key, 3)
        b, n, d, e, h = (4, 256, 512, 8, 1)
        x = jax.random.normal(k1, (b, n, d), dtype=jnp.float32)
        gate_w = jax.random.normal(k2, (h, d, e), dtype=jnp.float32)
        experts = jax.random.normal(k3, (e, d, d), dtype=jnp.float32) / np.sqrt(d)
        return {'x': x, 'gate_w': gate_w, 'experts': experts}
    _L0_ffn_all = _L0_ffn_setup()
    _L0_ffn_in = {k: v for k, v in _L0_ffn_all.items() if k in ('gate_w', 'experts')}
    del _L0_ffn_all
    return {'x': x, 'src': src, 'dst': dst, 'L0_gnn_W1': _L0_gnn_in['W1'], 'L0_gnn_att_src1': _L0_gnn_in['att_src1'], 'L0_gnn_att_dst1': _L0_gnn_in['att_dst1'], 'L0_gnn_b1': _L0_gnn_in['b1'], 'L0_gnn_W2': _L0_gnn_in['W2'], 'L0_gnn_att_src2': _L0_gnn_in['att_src2'], 'L0_gnn_att_dst2': _L0_gnn_in['att_dst2'], 'L0_gnn_b2': _L0_gnn_in['b2'], 'L0_gnn_fcW': _L0_gnn_in['fcW'], 'L0_gnn_fcb': _L0_gnn_in['fcb'], 'L0_ffn_gate_w': _L0_ffn_in['gate_w'], 'L0_ffn_experts': _L0_ffn_in['experts']}

def reference(x, src, dst, L0_gnn_W1, L0_gnn_att_src1, L0_gnn_att_dst1, L0_gnn_b1, L0_gnn_W2, L0_gnn_att_src2, L0_gnn_att_dst2, L0_gnn_b2, L0_gnn_fcW, L0_gnn_fcb, L0_ffn_gate_w, L0_ffn_experts):
    import jax
    import jax.numpy as jnp

    def _L0_gnn_ref(x, edge_index, W1, att_src1, att_dst1, b1, W2, att_src2, att_dst2, b2, fcW, fcb):
        import jax, jax.numpy as jnp
        import numpy as np
        N_NODES = 10000
        N_EDGES = 5000
        IN_DIM = 512
        HID = 256
        HEADS = 4
        OUT_DIM = 512
        NEG_SLOPE = 0.2

        def _glorot(key, shape):
            fan_in, fan_out = (shape[0], shape[-1])
            lim = jnp.sqrt(6.0 / (fan_in + fan_out))
            return jax.random.uniform(key, shape, jnp.float32, -lim, lim)

        def gat_conv(x, src, dst, W, att_src, att_dst, bias):
            N = x.shape[0]
            h = (x @ W).reshape(N, HEADS, HID)
            a_src = jnp.sum(h * att_src, axis=-1)
            a_dst = jnp.sum(h * att_dst, axis=-1)
            e = jax.nn.leaky_relu(a_src[src] + a_dst[dst], NEG_SLOPE)
            m = jax.ops.segment_max(e, dst, num_segments=N)
            e = jnp.exp(e - m[dst])
            s = jax.ops.segment_sum(e, dst, num_segments=N)
            alpha = e / (s[dst] + 1e-16)
            msg = alpha[:, :, None] * h[src]
            out = jax.ops.segment_sum(msg, dst, num_segments=N)
            return out.reshape(N, HEADS * HID) + bias
        N = x.shape[0]
        loops = jnp.arange(N, dtype=edge_index.dtype)
        src = jnp.concatenate([edge_index[0], loops])
        dst = jnp.concatenate([edge_index[1], loops])
        h = gat_conv(x, src, dst, W1, att_src1, att_dst1, b1)
        h = jax.nn.relu(h)
        h = gat_conv(h, src, dst, W2, att_src2, att_dst2, b2)
        h = jax.nn.relu(h)
        return h @ fcW + fcb

    def _L0_ffn_ref(x, gate_w, experts):
        import jax, jax.numpy as jnp
        import numpy as np
        SINKHORN_ITERS = 8
        TEMPERATURE = 1.0
        EPS = 1e-10

        def sinkhorn(gates):
            t = jnp.log(jnp.clip(gates, EPS)) / TEMPERATURE

            def body(t, _):
                t = t - jax.nn.logsumexp(t, axis=-2, keepdims=True)
                t = t - jax.nn.logsumexp(t, axis=-1, keepdims=True)
                return (t, None)
            t, _ = jax.lax.scan(body, t, None, length=SINKHORN_ITERS)
            return jnp.exp(t)
        b, n, d = x.shape
        h = gate_w.shape[0]
        e = experts.shape[0]
        N = b * n
        m = n // e
        x4 = x[:, None]
        gates = jnp.einsum('bhnd,hde->bhne', x4, gate_w)
        xf = jnp.transpose(x4, (1, 0, 2, 3)).reshape(h, N, d)
        gf = jnp.transpose(gates, (1, 0, 2, 3)).reshape(h, N, e)
        cg = sinkhorn(gf)
        vals, idx = jax.lax.top_k(jnp.transpose(cg, (0, 2, 1)), m)
        gate_values = (vals > 0.5).astype(x.dtype)
        gate_values = jnp.transpose(gate_values, (0, 2, 1))
        idx = jnp.transpose(idx, (0, 2, 1))
        routed = xf[jnp.arange(h)[:, None, None], idx]
        outputs = jnp.einsum('hmei,eio->hmeo', routed, experts)
        outputs = outputs * gate_values[..., None]
        o_dim = outputs.shape[-1]
        src = outputs.reshape(h, m * e, o_dim)
        idx_flat = idx.reshape(h, m * e)

        def combine(idxf, srcf):
            s = jnp.zeros((N, o_dim), srcf.dtype).at[idxf].add(srcf)
            c = jnp.zeros((N,), srcf.dtype).at[idxf].add(1.0)
            return s / (c + 1.0)[:, None]
        out = jax.vmap(combine)(idx_flat, src)
        out = out.reshape(h, b, n, o_dim)
        out = jnp.transpose(out, (1, 0, 2, 3))[:, 0]
        return out
    edge_index = jnp.stack([src, dst])
    x = x + _L0_gnn_ref(_layernorm(x, axis=-1), edge_index, L0_gnn_W1, L0_gnn_att_src1, L0_gnn_att_dst1, L0_gnn_b1, L0_gnn_W2, L0_gnn_att_src2, L0_gnn_att_dst2, L0_gnn_b2, L0_gnn_fcW, L0_gnn_fcb)
    x = x + _L0_ffn_ref(_layernorm(x, axis=-1)[None], L0_ffn_gate_w, L0_ffn_experts)[0]
    return x

_drawn_inputs = setup_inputs


def setup_inputs(seed=0):
    import zlib

    import numpy as np

    out = dict(_drawn_inputs(seed))
    spreads = {'L0_gnn_b1': (0.0, 0.1), 'L0_gnn_b2': (0.0, 0.1), 'L0_gnn_fcb': (0.0, 0.1)}
    factors = {}
    for name, (base, spread) in spreads.items():
        noise = np.random.default_rng([zlib.crc32(name.encode()), seed]).standard_normal(out[name].shape)
        drawn = base * np.exp(spread * noise) if base else spread * noise
        out[name] = jnp.asarray(drawn.astype(out[name].dtype))
    for name, factor in factors.items():
        out[name] = (out[name] * factor).astype(out[name].dtype)
    return out
```

```python
from contextlib import ExitStack

import concourse.bass as bass
from concourse import mybir

F32 = mybir.dt.float32
F32R = mybir.dt.float32r
BF16 = mybir.dt.bfloat16
I32 = mybir.dt.int32
ALU = mybir.AluOpType
ACT = mybir.ActivationFunctionType
AX = mybir.AxisListType.X

P = 128
N = 10000
E = 20000
D = 512
HEADS, HID = 4, 256
H = HEADS * HID
KD, KH = D // P, H // P
NT = (N + P - 1) // P
LAST = N - (NT - 1) * P
NPAD = NT * P
TT = 84
EC = 158
EROWS, EREST = E // EC, E % EC
PACKED = P * EC + 4 * P
NOWHERE = 1 << 20
C0, C1 = 128, 32
SLOPE = 0.2
BIG = 1e30
EXPERTS = 8
TOPK = N // EXPERTS
BLOCKS = (TOPK + P - 1) // P
LAST_ROWS = TOPK - (BLOCKS - 1) * P
EPS_LN = 1e-5
SINKHORN_ITERS = 8
GATE_MIN = 1e-10
FLOAT_BITS = 30


class Tile:

    def __init__(self, k, c):
        self.n = 2 * k + c
        self.h = k + c // 2
        self.s = c % 2

    def early(self, lag):
        return isinstance(self.n, int) and self.n < lag


def steps(eng, body, before, after=0, tiles=NT):
    def straight(i):
        def step(d):
            return Tile(i // 2, i % 2 + d) if 0 <= i + d < tiles else None
        body(step)

    lo, hi = 4, (tiles - 4) // 2 * 2
    for i in range(-before, lo):
        straight(i)
    with eng.Fori(lo // 2, hi // 2) as k:
        for c in range(2):
            body(lambda d, k=k, c=c: Tile(k, c + d))
    for i in range(hi, tiles + after):
        straight(i)


def gnn_ffn_kernel(nc, x, src, dst, W1, att_src1, att_dst1, b1, W2, att_src2, att_dst2, b2, fcW, fcb,
                   gate_w, experts, out):
    ctx = ExitStack()
    with ctx:
        def sb(name, shape, dt=F32):
            return ctx.enter_context(nc.sbuf_tensor(name, shape, dt))

        def sem(name):
            return ctx.enter_context(nc.semaphore(name))

        def dram(name, shape, dt=F32):
            return nc.dram_tensor(name, shape, dt, kind="Internal").ap()

        packed = dram("packed", (PACKED, 2), I32)
        h_rows = [dram(f"h_rows{n}", (NPAD, H)) for n in (1, 2)]
        xn_rows = dram("xn_rows", (N, D))
        att_rows = [dram(f"att_rows{n}", (NPAD, 2 * HEADS)) for n in (1, 2)]

        ps = [ctx.enter_context(nc.psum_tensor(f"ps{n}", [P, 1024], F32)) for n in range(4)]

        ident = sb("ident", [P, P])
        ones = sb("ones", [P, P])
        before = sb("before", [P, P])
        tile_base = sb("tile_base", [P, TT])
        node_id = sb("node_id", [P, TT])
        iota = sb("iota", [P, P])
        wa_hi = [sb(f"wa{n}_hi", [P, k, 2 * HEADS], F32R) for n, k in ((1, KD), (2, KH))]
        wa_lo = [sb(f"wa{n}_lo", [P, k, 2 * HEADS], F32R) for n, k in ((1, KD), (2, KH))]
        att = [sb(f"att{n}", [P, TT, 2 * HEADS]) for n in (1, 2)]
        self_count = sb("self_count", [P, TT])
        gates = sb("gates", [P, NT, EXPERTS])
        table = sb("table", [1, 3, TT], I32)

        gat_weights = ExitStack()

        def sbw(name, shape, dt=F32):
            return gat_weights.enter_context(nc.sbuf_tensor(name, shape, dt))

        wA_hi = sbw("wA_hi", [P, KD * H], F32R)
        wA_lo = sbw("wA_lo", [P, KD * H], F32R)
        wB_hi = sbw("wB_hi", [P, KH * H], F32R)
        wB_lo = sbw("wB_lo", [P, KH * H], F32R)

        early = ExitStack()

        def sbe(name, shape, dt=F32):
            return early.enter_context(nc.sbuf_tensor(name, shape, dt))

        stage = sbe("stage", [P, 2, 2048])
        att_vec = sbe("att_vec", [P, 2, H])
        prod = sbe("prod", [P, 2048])
        wa_f = sbe("wa_f", [P, KH, 2 * HEADS])
        e_src = sbe("e_src", [P, EC], I32)
        e_dst = sbe("e_dst", [P, EC], I32)
        e_hi = sbe("e_hi", [P, EC])
        e_lo = sbe("e_lo", [P, EC])
        e_tmp = sbe("e_tmp", [P, EC], I32)
        e_other = sbe("e_other", [P, EC])
        e_self = sbe("e_self", [P, EC])
        e_count = sbe("e_count", [P, EC])
        e_pos = sbe("e_pos", [P, EC], I32)
        e_row = sbe("e_row", [P, EC, 2], I32)
        nowhere = sbe("nowhere", [P, 2 * EC], I32)
        zeros_e = sbe("zeros_e", [P, EC])
        before_me = sbe("before_me", [P, 1])
        pos_col = sbe("pos_col", [P, 4, 1], I32)
        row_col = sbe("row_col", [P, 4, 2], I32)
        hot_lo = sbe("hot_lo", [P, 4, P], BF16)
        hot_hi = sbe("hot_hi", [P, 4, 2 * TT], BF16)
        zero_b = sbe("zero_b", [P, 2 * TT], BF16)
        other_count = sbe("other_count", [P, TT])
        tile_sum = sbe("tile_sum", [P, TT])
        tile_scan = sbe("tile_scan", [P, TT])
        loops_f = sbe("loops_f", [1, TT])
        loops_i = sbe("loops_i", [1, TT], I32)
        loops_scan = sbe("loops_scan", [1, TT])
        x_in = sbe("x_in", [P, 2, D])
        x_norm = sbe("x_norm", [P, 2, D])
        ln_stats = sbe("ln_stats", [P, 2, 6])
        ln_mv = sbe("ln_mv", [P, 2, 2])
        ln_std = sbe("ln_std", [P, 2, 1])
        ln_rstd = sbe("ln_rstd", [P, 2, 1])
        ln_step = sbe("ln_step", [P, 2, 1])
        eps_col = sbe("eps_col", [P, 1])
        xT_hi = sbe("xT_hi", [P, 2, D], F32R)
        xT_lo = sbe("xT_lo", [P, 2, D], F32R)
        h_out = sbe("h_out", [P, 2, H])

        consts = sem("consts")
        cleared = sem("cleared")
        edges_in = sem("edges_in")
        w_in = [sem("w_in0"), sem("w_in1")]
        w_hi_done = sem("w_hi_done")
        w_lo_done = sem("w_lo_done")
        att_in = [sem("att_in1"), sem("att_in2")]
        fill_done = sem("fill_done")
        parts_ready = sem("parts_ready")
        parts_summed = sem("parts_summed")
        rows_ready = sem("rows_ready")
        col_copied = sem("col_copied")
        scattered = [sem(f"scattered{n}") for n in range(4)]
        hot_ready = sem("hot_ready")
        hot_used = sem("hot_used")
        counts_done = sem("counts_done")
        table_done = sem("table_done")
        x_got = [sem("x_got0"), sem("x_got1")]
        std_ready = sem("std_ready")
        mv_ready = sem("mv_ready")
        xn_ready = sem("xn_ready")
        xt_ready = sem("xt_ready")
        xhi_ready = sem("xhi_ready")
        xlo_ready = sem("xlo_ready")
        h1_ready = sem("h1_ready")
        h1_left = sem("h1_left")
        h1_right = sem("h1_right")
        h1_stored = [sem("h1_stored0"), sem("h1_stored1")]
        att_stored = sem("att_stored")
        early.close()

        gat = ExitStack()

        def sbg(name, shape, dt=F32):
            return gat.enter_context(nc.sbuf_tensor(name, shape, dt))

        ix = sbg("ix", [P, 2, 2, 2], I32)
        dst_row = sbg("dst_row", [P, 2, C0 + C1, 2], I32)
        at_tile = sbg("at_tile", [P, 2, 2])
        off_tile = sbg("off_tile", [P, 2, 2])
        drop = sbg("drop", [P, 2, 2])
        src_ok = sbg("src_ok", [P, 2, 2, 1], I32)
        near_att = sbg("near_att", [P, 2, 2, 2 * HEADS])
        near_h = [sbg(f"near_h{c}", [P, 2, H]) for c in range(2)]
        diag = [sbg("diag0", [P, HEADS, C0]), sbg("diag1", [P, HEADS, C1])]
        hot_t = sbg("hot_t", [P, 2 * P])
        miss = sbg("miss", [P, C0 + C1])
        seen = sbg("seen", [P, HEADS, C0 + C1])
        hot = sbg("hot", [P, 2, P])
        hot1 = sbg("hot1", [P, 2, P])
        top = sbg("top", [P, HEADS])
        m_top = sbg("m_top", [P, HEADS])
        maxima = sbg("maxima", [P, 2 * HEADS])
        e_in = sbg("e_in", [P, 2, HEADS])
        e_own = sbg("e_own", [P, 2, HEADS])
        weight = sbg("weight", [P, 2, HEADS])
        weight_own = sbg("weight_own", [P, 2, HEADS])
        message = [sbg(f"message{c}", [P, H]) for c in range(2)]
        own = sbg("own", [P, 2, H])
        own_msg = sbg("own_msg", [P, H])
        total = sbg("total", [P, H])
        denom = sbg("denom", [P, HEADS])
        gathered = sbg("gathered", [P, H])
        act_hi = sbg("act_hi", [P, H], F32R)
        act_lo = sbg("act_lo", [P, H], F32R)
        result = sbg("result", [P, 2, H])
        bias_row = sbg("bias_row", [P, H])
        m_ix = sbg("m_ix", [P, 2], I32)
        m_row = sbg("m_row", [P, P, 2], I32)
        m_small = sbg("m_small", [P, 2])
        m_src = sbg("m_src", [P, 1], I32)
        m_att = sbg("m_att", [P, 2 * HEADS])
        m_diag = sbg("m_diag", [P, HEADS, P])
        m_miss = sbg("m_miss", [P, P])
        x_ix = sbg("x_ix", [P, 2], I32)
        x_row = sbg("x_row", [P, P, 2], I32)
        x_small = sbg("x_small", [P, 3])
        x_src = sbg("x_src", [P, 1], I32)
        x_att = sbg("x_att", [P, 2 * HEADS])
        x_h = sbg("x_h", [P, H])
        x_hot_t = sbg("x_hot_t", [P, P])
        x_hot = sbg("x_hot", [P, P])
        x_e = sbg("x_e", [P, HEADS])
        x_weight = sbg("x_weight", [P, HEADS])
        x_msg = sbg("x_msg", [P, H])
        x_again = sbg("x_again", [P, D])
        fcb_row = sbg("fcb_row", [P, D])
        x_plus = sbg("x_plus", [P, D])
        ln2 = sbg("ln2", [P, 16])
        xT = sbg("xT", [P, D])
        gate_cols = sbg("gate_cols", [P, KD, EXPERTS])
        half_neg = sbg("half_neg", [P, 1])

        phase = sem("phase")
        fc_in = [sem("fc_in0"), sem("fc_in1")]
        fc_hi = sem("fc_hi")
        fc_lo = sem("fc_lo")
        small_in = sem("small_in")

        class Layer:

            def __init__(self, n):
                def s(name):
                    return sem(f"{name}_{n}")
                self.listed = [s("listed0"), s("listed1")]
                self.src_ready = s("src_ready")
                self.att_got = [s("att_got0"), s("att_got1")]
                self.h_got = [s("h_got0"), s("h_got1")]
                self.own_got = [s("own_got0"), s("own_got1")]
                self.diag_ready = s("diag_ready")
                self.spread = s("spread")
                self.max_ready = s("max_ready")
                self.at_edges = s("at_edges")
                self.e_ready = s("e_ready")
                self.msg_ready = s("msg_ready")
                self.own_ready = s("own_ready")
                self.summed = s("summed")
                self.denom_read = s("denom_read")
                self.gathered_ready = s("gathered_ready")
                self.turned = s("turned")
                self.hi_ready = s("hi_ready")
                self.lo_ready = s("lo_ready")
                self.first_done = s("first_done")
                self.second_done = s("second_done")
                self.copied = s("copied")
                self.extra_read = s("extra_read")
                self.stored = [s("stored0"), s("stored1")]
                self.m_listed = s("m_listed")
                self.m_src_ready = s("m_src_ready")
                self.m_got = s("m_got")
                self.m_diag_ready = s("m_diag_ready")
                self.m_spread = s("m_spread")
                self.m_used = s("m_used")
                self.x_listed = s("x_listed")
                self.x_src_ready = s("x_src_ready")
                self.x_got = s("x_got")
                self.x_at_edges = s("x_at_edges")
                self.x_e_ready = s("x_e_ready")
                self.x_msg_ready = s("x_msg_ready")
                self.x_used = s("x_used")

        layers = [Layer(1), Layer(2)]
        bias_in = sem("bias_in")
        x_again_got = sem("x_again_got")
        x_plus_ready = sem("x_plus_ready")
        var_ready = sem("var_ready")
        pow_ready = sem("pow_ready")
        xn2_ready = sem("xn2_ready")
        xn2_turned = sem("xn2_turned")
        xT_ready = sem("xT_ready")
        gates_done = sem("gates_done")
        gat.close()
        gat_weights.close()

        route = ExitStack()

        def sbr(name, shape, dt=F32):
            return route.enter_context(nc.sbuf_tensor(name, shape, dt))

        NB = EXPERTS * BLOCKS
        ew_hi = sbr("ew_hi", [P, EXPERTS, KD, D], F32R)
        ew_lo = sbr("ew_lo", [P, EXPERTS, KD, D], F32R)
        ew_in = sbr("ew_in", [P, 2, KD, D])
        logp = sbr("logp", [P, NT, EXPERTS])
        work = sbr("work", [P, NT, EXPERTS])
        prob = sbr("prob", [P, NT, EXPERTS])
        above = sbr("above", [P, NT, EXPERTS])
        tie = sbr("tie", [P, NT, EXPERTS])
        above_b = sbr("above_b", [P, NT, EXPERTS], BF16)
        tie_b = sbr("tie_b", [P, NT, EXPERTS], BF16)
        scan = sbr("scan", [P, NT, EXPERTS])
        place = sbr("place", [P, NT, EXPERTS])
        place_i = sbr("place_i", [P, NT, EXPERTS], I32)
        place_hi = sbr("place_hi", [P, NT, EXPERTS])
        place_lo = sbr("place_lo", [P, NT, EXPERTS])
        code = sbr("code", [P, NT, EXPERTS])
        row_a = sbr("row_a", [P, NT])
        row_b = sbr("row_b", [P, NT])
        outside = sbr("outside", [P, NT])
        inside = sbr("inside", [P, 1])
        outside_neg = sbr("outside_neg", [P, 1])
        tile_no = sbr("tile_no", [P, NT])
        ones_b = sbr("ones_b", [P, P], BF16)
        before_b = sbr("before_b", [P, P], BF16)
        col_a = sbr("col_a", [P, EXPERTS])
        col_b = sbr("col_b", [P, EXPERTS])
        col_c = sbr("col_c", [P, EXPERTS])
        col_t = sbr("col_t", [EXPERTS, 1])
        col_diag = sbr("col_diag", [EXPERTS, EXPERTS])
        bit = sbr("bit", [P, EXPERTS], I32)
        found = sbr("found", [P, EXPERTS], I32)
        trial = sbr("trial", [P, EXPERTS], I32)
        zeros_r = sbr("zeros_r", [P, NT])
        zero_rb = sbr("zero_rb", [P, EXPERTS * 3 * BLOCKS], BF16)
        place_hot = sbr("place_hot", [P, 2, EXPERTS, P], BF16)
        block_hot = sbr("block_hot", [P, 2, EXPERTS, BLOCKS])
        block_val = sbr("block_val", [P, 2, EXPERTS, 3, BLOCKS], BF16)
        listed_f = sbr("listed_f", [P, EXPERTS, 3, BLOCKS])
        token_f = sbr("token_f", [P, EXPERTS, BLOCKS])
        token = sbr("token", [P, NB, 1], I32)
        factor = sbr("factor", [P, NB, 1])
        past_end = sbr("past_end", [P, 1])
        expert_of = sbr("expert_of", [1, NB], I32)
        fetch_at = sbr("fetch_at", [P, 2, 1], I32)
        add_at = sbr("add_at", [P, 2, 1], I32)
        x_tok = ew_in[:, 0, 0:2, :]
        y_tok = ew_in[:, 0, 2:4, :]
        tT_hi = sbr("tT_hi", [P, 2, D], F32R)
        tT_lo = sbr("tT_lo", [P, 2, D], F32R)

        ew_got = [sem("ew_got0"), sem("ew_got1")]
        ew_hi_done = sem("ew_hi_done")
        ew_lo_done = sem("ew_lo_done")
        to_log = sem("to_log")
        from_log = sem("from_log")
        share_ready = sem("share_ready")
        share_done = sem("share_done")
        hots_ready = sem("hots_ready")
        hots_used = sem("hots_used")
        lists_ready = sem("lists_ready")
        fetch_ready = sem("fetch_ready")
        tok_got = [sem("tok_got0"), sem("tok_got1")]
        tok_turned = sem("tok_turned")
        tok_hi = sem("tok_hi")
        tok_lo = sem("tok_lo")
        tok_done = sem("tok_done")
        add_ready = sem("add_ready")
        y_ready = sem("y_ready")
        added = sem("added")
        route.close()

        passed = sem("passed")

        block = ctx.enter_context(nc.Block())

        W_PIECES = [(W1, 0, p) for p in range(2)] + [(W2, 1, p) for p in range(4)]

        def w_view(w, piece):
            return w.rearrange("(k p) n -> p k n", p=P)[:, 2 * piece:2 * piece + 2, :]


        def more_chunks(eng, t, body):
            count = eng.value_load(table[0:1, 1, bass.ds(t.n, 1)], min_val=0, max_val=E // P + 1)
            with eng.If(count > 0):
                before_it = eng.value_load(table[0:1, 2, bass.ds(t.n, 1)], min_val=0, max_val=E // P + 1)
                with eng.Fori(0, count) as j:
                    body(before_it + j, j)

        @block.sync
        def _(sp):
            sp.wait_ge(cleared, 2)
            for e, given in ((e_src, src), (e_dst, dst)):
                sp.dma_start(e[0:EROWS, :], given[0:EROWS * EC].rearrange("(p j) -> p j", j=EC)).then_inc(edges_in, 16)
                sp.dma_start(e[EROWS:EROWS + 1, 0:EREST], given[EROWS * EC:E].rearrange("(o j) -> o j", o=1)).then_inc(edges_in, 16)
            for n, (w, layer, piece) in enumerate(W_PIECES):
                if n >= 2:
                    sp.wait_ge(w_hi_done, n - 1)
                    sp.wait_ge(w_lo_done, n - 1)
                sp.dma_start(stage[:, n % 2, :].rearrange("p (k n) -> p k n", k=2), w_view(w, piece)).then_inc(w_in[n % 2], 16)
                if piece == 0:
                    if layer == 1:
                        sp.wait_ge(w_lo_done, 2)
                    for m, a in enumerate(((att_src1, att_dst1), (att_src2, att_dst2))[layer]):
                        sp.dma_start(att_vec[:, m, :], a.rearrange("(o h) c -> o (h c)", o=1).to_broadcast((P, H))).then_inc(att_in[layer], 16)

            def store_h1(t):
                if t is None:
                    return
                sp.wait_ge(h1_left, t.n + 1)
                sp.wait_ge(h1_right, t.n + 1)
                sp.dma_start(h_rows[0][bass.ds(t.n * P, P), :], h_out[:, t.s, :]).then_inc(h1_stored[t.s], 16)

            def load_x(t):
                if t is None:
                    return
                if not t.early(2):
                    sp.wait_ge(xn_ready, t.n - 1)
                rows = P if not (isinstance(t.n, int) and t.n == NT - 1) else LAST
                sp.dma_start(x_in[0:rows, t.s, :], x[bass.ds(t.n * P, rows), :]).then_inc(x_got[t.s], 16)

            def step(s):
                store_h1(s(-1))
                load_x(s(3))
            steps(sp, step, 3, 1)
            sp.dma_start(att_rows[0].rearrange("(t p) a -> p t a", p=P), att[0][:, 0:NT, :]).then_inc(att_stored, 16)
            for n in range(2):
                sp.wait_ge(h1_stored[n], 16 * ((NT + 1 - n) // 2))
            sp.wait_ge(att_stored, 16)
            sp.sem_inc(phase, 1)
            sp.wait_ge(phase, 5)

            for n in range(4):
                if n >= 2:
                    sp.wait_ge(fc_hi, n - 1)
                    sp.wait_ge(fc_lo, n - 1)
                sp.dma_start(own[:, n % 2, :].rearrange("p (k n) -> p k n", k=2),
                             fcW.rearrange("(k p) n -> p k n", p=P)[:, 2 * n:2 * n + 2, :]).then_inc(fc_in[n % 2], 16)
            sp.dma_start(fcb_row[:], fcb.rearrange("(o n) -> o n", o=1).to_broadcast((P, D))).then_inc(small_in, 16)
            sp.dma_start(gate_cols[:], gate_w[0].rearrange("(k p) e -> p k e", p=P)).then_inc(small_in, 16)
            sp.wait_ge(fc_lo, 4)

            def gat_layer(n, L):
                sp.dma_start(bias_row[:], (b1, b2)[n].rearrange("(o n) -> o n", o=1).to_broadcast((P, H))).then_inc(bias_in, 16)

                def lists(t):
                    if t is None:
                        return
                    first = sp.value_load(table[0:1, 0, bass.ds(t.n, 1)], min_val=0, max_val=E)
                    if not t.early(2):
                        sp.wait_ge(L.max_ready, t.n - 1)
                    rows = packed[bass.ds(first, 2 * P), :]
                    sp.dma_start(ix[:, t.s, :, :], rows.rearrange("(c p) w -> p c w", p=P)).then_inc(L.listed[t.s], 16)
                    sp.dma_start(dst_row[:, t.s, :, :].rearrange("p e w -> p (e w)"),
                                 packed[bass.ds(first, C0 + C1), :].rearrange("(o e) w -> o (e w)", o=1).to_broadcast((P, 2 * (C0 + C1)))).then_inc(L.listed[t.s], 16)

                def own_rows(t):
                    if t is None:
                        return
                    if not t.early(2):
                        sp.wait_ge(L.gathered_ready, t.n - 1)
                    sp.dma_start(own[:, t.s, :], h_rows[n][bass.ds(t.n * P, P), :]).then_inc(L.own_got[t.s], 16)

                def x_rows(t):
                    if t is None or n == 0:
                        return
                    if not t.early(1):
                        sp.wait_ge(x_plus_ready, t.n)
                    elif t.early(1):
                        sp.wait_ge(consts, 2)
                    rows = P if not (isinstance(t.n, int) and t.n == NT - 1) else LAST
                    sp.dma_start(x_again[0:rows, :], x[bass.ds(t.n * P, rows), :]).then_inc(x_again_got, 16)

                def more_lists(t, to, listed, used):
                    if t is None:
                        return

                    def body(v, j):
                        first = sp.value_load(table[0:1, 0, bass.ds(t.n, 1)], min_val=0, max_val=E)
                        start = nc.s_assert_within(first + j * P + (C0 + C1), 0, E + P, skip_runtime_bounds_check_because="a tile's chunks end at most a chunk past the last edge")
                        rows = packed[bass.ds(start, P), :]
                        sp.wait_ge(used, v + 1)
                        sp.dma_start(to[0][:], rows).then_inc(listed, 16)
                        sp.dma_start(to[1][:].rearrange("p e w -> p (e w)"),
                                     rows.rearrange("(o e) w -> o (e w)", o=1).to_broadcast((P, 2 * P))).then_inc(listed, 16)
                    more_chunks(sp, t, body)

                def store(t):
                    if t is None:
                        return
                    if n == 0:
                        sp.wait_ge(L.copied, 2 * (t.n + 1))
                        sp.dma_start(h_rows[1][bass.ds(t.n * P, P), :], result[:, t.s, :]).then_inc(L.stored[t.s], 16)
                    else:
                        sp.wait_ge(xn2_ready, t.n + 1)
                        rows = P if not (isinstance(t.n, int) and t.n == NT - 1) else LAST
                        sp.dma_start(out[bass.ds(t.n * P, rows), :], result[0:rows, t.s, 0:D]).then_inc(L.stored[t.s], 16)
                        sp.dma_start(xn_rows[bass.ds(t.n * P, rows), :], result[0:rows, t.s, D:2 * D]).then_inc(L.stored[t.s], 16)

                def step(s):
                    more_lists(s(1), (x_ix, x_row), L.x_listed, L.x_used)
                    more_lists(s(2), (m_ix, m_row), L.m_listed, L.m_used)
                    own_rows(s(2))
                    x_rows(s(1))
                    store(s(-1))
                    lists(s(4))
                steps(sp, step, 4, 1)
                for m in range(2):
                    sp.wait_ge(L.stored[m], 16 * (n + 1) * ((NT + 1 - m) // 2))
                if n == 0:
                    sp.wait_ge(L.extra_read, NT)
                    sp.dma_start(att_rows[1].rearrange("(t p) a -> p t a", p=P), att[1][:, 0:NT, :]).then_inc(att_stored, 16)
                    sp.wait_ge(att_stored, 32)
                sp.sem_inc(phase, 1)
                sp.wait_ge(phase, 10 + 5 * n)
            gat_layer(0, layers[0])
            gat_layer(1, layers[1])
            for e in range(EXPERTS):
                if e >= 2:
                    sp.wait_ge(ew_hi_done, e - 1)
                    sp.wait_ge(ew_lo_done, e - 1)
                sp.dma_start(ew_in[:, e % 2, :, :], experts[e].rearrange("(k p) n -> p k n", p=P)).then_inc(ew_got[e % 2], 16)
            sp.wait_ge(added, 16 * NB)

        @block.gpsimd
        def _(pool):
            pool.memset(e_src[:], NOWHERE).then_inc(cleared, 1)
            pool.memset(e_dst[:], NOWHERE).then_inc(cleared, 1)
            pool.memset(ident[:], 0.0)
            pool.memset(ones[:], 1.0)
            pool.memset(before[:], 1.0)
            pool.memset(zero_b[:], 0.0)
            pool.memset(zeros_e[:], 0.0)
            pool.memset(eps_col[:], EPS_LN)
            pool.iota(iota[:], pattern=[[1, P]], base=0, channel_multiplier=0, allow_small_or_imprecise_dtypes=True)
            pool.iota(tile_base[:], pattern=[[P, TT]], base=0, channel_multiplier=0, allow_small_or_imprecise_dtypes=True)
            pool.iota(node_id[:], pattern=[[P, TT]], base=0, channel_multiplier=1, allow_small_or_imprecise_dtypes=True)
            pool.drain()
            pool.affine_select(out=ident[:], in_=ident[:], compare_op=ALU.not_equal, fill=1.0, base=0,
                               pattern=[[-1, P]], channel_multiplier=1)
            pool.affine_select(out=before[:], in_=before[:], compare_op=ALU.is_gt, fill=0.0, base=0,
                               pattern=[[1, P]], channel_multiplier=-1)
            pool.drain().then_inc(consts, 1)

            pool.memset(nowhere[:], NOWHERE)
            pool.drain()
            pool.dma_start(packed[0:P * EC, :].rearrange("(p j) w -> p (j w)", p=P), nowhere[:]).then_inc(fill_done, 16)
            pool.dma_start(packed[P * EC:PACKED, :].rearrange("(p j) w -> p (j w)", p=P), nowhere[:, 0:8]).then_inc(fill_done, 16)
            pool.wait_ge(fill_done, 32)
            pool.wait_ge(rows_ready, 1)

            packed_end = pool.to_reg(PACKED - 1)

            def scatter(k, c, wait):
                slot = c % 4
                if wait is not None:
                    pool.wait_ge(scattered[slot], wait)
                    pool.sem_inc(passed, 1)
                pool.tensor_copy(pos_col[:, slot, :], e_pos[:, bass.ds(2 * k + c, 1)]).then_inc(col_copied, 1)
                pool.tensor_copy(row_col[:, slot, :], e_row[:, bass.ds(2 * k + c, 1), :].rearrange("p o w -> p (o w)")).then_inc(col_copied, 1)
                pool.wait_ge(col_copied, 2 * (2 * k + c) + 2)
                pool.sem_inc(passed, 1)
                pool.indirect_dma_start(out=packed, out_offset=bass.IndirectOffsetOnAxis(ap=pos_col[:, slot, :], axis=0),
                                        in_=row_col[:, slot, :], in_offset=None, bounds_check=packed_end, oob_is_err=False).then_inc(scattered[slot], 16)
            for c in range(4):
                scatter(0, c, None)
            with pool.Fori(1, EC // 4) as q:
                for c in range(4):
                    scatter(2 * q, c, 16 * q)
            for c in range(EC - EC // 4 * 4):
                scatter(2 * (EC // 4), c, 16 * (EC // 4))

            for m in range(4):
                pool.wait_ge(scattered[m], 16 * ((EC + 3 - m) // 4))
            pool.drain().then_inc(phase, 1)
            pool.wait_ge(phase, 5)
            for m in range(2):
                pool.memset(near_h[m][:], 0.0)
            pool.memset(near_att[:], 0.0)
            pool.memset(hot_t[:], 0.0)
            pool.memset(m_att[:], 0.0)
            pool.memset(x_att[:], 0.0)
            pool.memset(x_h[:], 0.0)
            pool.memset(half_neg[:], -0.5)
            pool.memset(x_again[:], 0.0)
            pool.drain().then_inc(consts, 1)
            nodes_end = pool.to_reg(NPAD - 1)

            def gat_layer(n, L):
                def fetch(to, rows_of, index, got):
                    pool.indirect_dma_start(out=to, out_offset=None, in_=rows_of,
                                            in_offset=bass.IndirectOffsetOnAxis(ap=index, axis=0),
                                            bounds_check=nodes_end, oob_is_err=False).then_inc(got, 16)

                def spread_diag(to, terms, rows):
                    one = ident[0:rows, 0:to.shape[2]].rearrange("p (o e) -> p o e", o=1).to_broadcast((rows, HEADS, to.shape[2]))
                    return pool.tensor_tensor(to[0:rows, :, :], one, terms.rearrange("p (h o) -> p h o", o=1).to_broadcast((rows, HEADS, to.shape[2])), ALU.mult)

                def gathers(t):
                    if t is None:
                        return
                    if not t.early(2):
                        pool.wait_ge(L.msg_ready, t.n - 1)
                        pool.sem_inc(passed, 1)
                    pool.wait_ge(L.src_ready, t.n + 1)
                    pool.sem_inc(passed, 1)
                    fetch(near_att[:, t.s, 0, :], att_rows[n], src_ok[:, t.s, 0, :], L.att_got[t.s])
                    fetch(near_att[0:C1, t.s, 1, :], att_rows[n], src_ok[0:C1, t.s, 1, :], L.att_got[t.s])
                    fetch(near_h[0][:, t.s, :], h_rows[n], src_ok[:, t.s, 0, :], L.h_got[t.s])
                    fetch(near_h[1][0:C1, t.s, :], h_rows[n], src_ok[0:C1, t.s, 1, :], L.h_got[t.s])

                def diagonals(t):
                    if t is None:
                        return
                    pool.wait_ge(L.att_got[t.s], 32 * (t.h + 1))
                    if not t.early(1):
                        pool.wait_ge(L.spread, t.n)
                    pool.sem_inc(passed, 1)
                    spread_diag(diag[0], near_att[:, t.s, 0, 0:HEADS], C0)
                    spread_diag(diag[1], near_att[0:C1, t.s, 1, 0:HEADS], C1)
                    pool.sem_inc(passed, 1)
                    pool.engine_nop().then_inc(L.diag_ready, 1)

                def own_messages(t):
                    if t is None:
                        return
                    pool.wait_ge(L.own_got[t.s], 16 * (t.h + 1))
                    pool.wait_ge(L.msg_ready, t.n + 1)
                    if not t.early(1):
                        pool.wait_ge(L.gathered_ready, t.n)
                    pool.sem_inc(passed, 1)
                    pool.tensor_tensor(own_msg[:].rearrange("p (h c) -> p h c", h=HEADS), own[:, t.s, :].rearrange("p (h c) -> p h c", h=HEADS),
                                       weight_own[:, t.s, :].rearrange("p (h o) -> p h o", o=1).to_broadcast((P, HEADS, HID)), ALU.mult).then_inc(L.own_ready, 1)

                def m_body(v, j):
                    pool.wait_ge(L.m_src_ready, v + 1)
                    pool.sem_inc(passed, 1)
                    fetch(m_att[:], att_rows[n], m_src[:], L.m_got)
                    pool.wait_ge(L.m_got, 16 * (v + 1))
                    pool.sem_inc(passed, 1)
                    spread_diag(m_diag, m_att[:, 0:HEADS], P).then_inc(L.m_diag_ready, 1)

                def x_body(v, j):
                    pool.wait_ge(L.x_src_ready, v + 1)
                    pool.sem_inc(passed, 1)
                    fetch(x_att[:], att_rows[n], x_src[:], L.x_got)
                    fetch(x_h[:], h_rows[n], x_src[:], L.x_got)

                def plus(t):
                    if t is None or n == 0:
                        return
                    pool.wait_ge(x_again_got, 16 * (t.n + 1))
                    if not t.early(1):
                        pool.wait_ge(var_ready, t.n)
                    else:
                        pool.wait_ge(small_in, 32)
                    pool.sem_inc(passed, 1)
                    pool.tensor_tensor(x_plus[:], x_again[:], fcb_row[:], ALU.add).then_inc(x_plus_ready, 1)

                def power(t):
                    if t is None or n == 0:
                        return
                    pool.wait_ge(var_ready, t.n + 1)
                    pool.sem_inc(passed, 1)
                    pool.tensor_tensor(ln2[:, 9:10], ln2[:, 8:9], half_neg[:], ALU.pow).then_inc(pow_ready, 1)

                def step(s):
                    if s(1) is not None:
                        more_chunks(pool, s(1), x_body)
                    diagonals(s(2))
                    if s(2) is not None:
                        more_chunks(pool, s(2), m_body)
                    power(s(-1))
                    own_messages(s(1))
                    plus(s(0))
                    gathers(s(3))
                steps(pool, step, 3, 1)
                pool.drain().then_inc(phase, 1)
                pool.wait_ge(phase, 10 + 5 * n)
            gat_layer(0, layers[0])
            gat_layer(1, layers[1])
            pool.memset(ones_b[:], 1.0)
            pool.memset(zeros_r[:], 0.0)
            pool.memset(zero_rb[:], 0.0)
            pool.memset(bit[:], 1 << (FLOAT_BITS - 1))
            pool.memset(found[:], 0)
            pool.tensor_copy(before_b[:], before[:])
            pool.iota(expert_of[:], pattern=[[1, EXPERTS], [0, BLOCKS]], base=0, channel_multiplier=0)
            pool.tensor_scalar(outside[:], node_id[:, 0:NT], float(N), None, ALU.is_ge)
            pool.tensor_scalar(inside[:], node_id[:, NT - 1:NT], float(N), None, ALU.is_lt)
            pool.tensor_scalar(outside_neg[:], node_id[:, NT - 1:NT], float(N), -BIG, ALU.is_ge, ALU.mult)
            pool.tensor_scalar(past_end[:], node_id[:, 0:1], float(LAST_ROWS), None, ALU.is_ge)
            pool.tensor_scalar(tile_no[:], tile_base[:, 0:NT], 1.0 / P, None, ALU.mult)
            pool.drain().then_inc(consts, 1)
            for e in range(EXPERTS):
                pool.wait_ge(ew_hi_done, e + 1)
                pool.tensor_tensor(ew_lo[:, e, :, :], ew_in[:, e % 2, :, :], ew_hi[:, e, :, :].bitcast(F32), ALU.subtract).then_inc(ew_lo_done, 1)
            tokens_end = pool.to_reg(N - 1)
            pool.wait_ge(ew_lo_done, EXPERTS)

            def fetch(t):
                if t is None:
                    return
                if not t.early(2):
                    pool.wait_ge(tok_turned, t.n - 1)
                    pool.sem_inc(passed, 1)
                pool.wait_ge(fetch_ready, t.n + 1)
                pool.sem_inc(passed, 1)
                pool.indirect_dma_start(out=x_tok[:, t.s, :], out_offset=None, in_=xn_rows,
                                        in_offset=bass.IndirectOffsetOnAxis(ap=fetch_at[:, t.s, :], axis=0),
                                        bounds_check=tokens_end, oob_is_err=False).then_inc(tok_got[t.s], 16)

            def add(t):
                if t is None:
                    return
                pool.wait_ge(y_ready, t.n + 1)
                pool.wait_ge(add_ready, t.n + 1)
                if not t.early(1):
                    pool.wait_ge(added, 16 * t.n)
                pool.sem_inc(passed, 1)
                pool.indirect_dma_start(out=out, out_offset=bass.IndirectOffsetOnAxis(ap=add_at[:, t.s, :], axis=0),
                                        in_=y_tok[:, t.s, :], in_offset=None, bounds_check=tokens_end, oob_is_err=True,
                                        compute_op=ALU.add).then_inc(added, 16)

            def step(s):
                fetch(s(2))
                add(s(-1))
            steps(pool, step, 2, 1, NB)

        @block.scalar
        def _(act):
            for n, (w, layer, piece) in enumerate(W_PIECES):
                act.wait_ge(w_in[n % 2], 16 * (n // 2 + 1))
                hi = (wA_hi, wB_hi)[layer]
                act.activation(hi[:, piece * 2048:(piece + 1) * 2048], stage[:, n % 2, :], ACT.Copy).then_inc(w_hi_done, 1)
            act.wait_ge(consts, 1)

            def deviation(t):
                if t is None:
                    return
                act.wait_ge(mv_ready, t.n + 1)
                act.activation(ln_std[:, t.s, :], ln_mv[:, t.s, 1:2], ACT.Sqrt, bias=eps_col[:, 0:1]).then_inc(std_ready, 1)

            def high(t):
                if t is None:
                    return
                act.wait_ge(xt_ready, t.n + 1)
                if not t.early(2):
                    act.wait_ge(h1_ready, t.n - 1)
                act.activation(xT_hi[:, t.s, :], ps[1][:, t.s * 512:t.s * 512 + 512], ACT.Copy).then_inc(xhi_ready, 1)

            def left(t):
                if t is None:
                    return
                act.wait_ge(h1_ready, t.n + 1)
                if not t.early(2):
                    act.wait_ge(h1_stored[t.s], 16 * t.h)
                act.activation(h_out[:, t.s, 0:512], ps[2 * t.s][:, 0:512], ACT.Copy).then_inc(h1_left, 1)

            def step(s):
                left(s(-1))
                deviation(s(2))
                high(s(1))
            steps(act, step, 2, 1)
            act.drain().then_inc(phase, 1)
            act.wait_ge(phase, 5)
            for n in range(4):
                act.wait_ge(fc_in[n % 2], 16 * (n // 2 + 1))
                act.activation(wA_hi[:, n * 1024:(n + 1) * 1024], own[:, n % 2, :], ACT.Copy).then_inc(fc_hi, 1)

            def gat_layer(n, L):
                def by_head(to, rows, h, w):
                    for m in range(HEADS):
                        act.activation(to[0:rows, m * HID:(m + 1) * HID], h[0:rows, m * HID:(m + 1) * HID], ACT.Copy, scale=w[0:rows, m:m + 1])

                def high(t):
                    if t is None:
                        return
                    act.wait_ge(L.turned, t.n + 1)
                    if not t.early(1):
                        act.wait_ge(L.second_done, t.n)
                    act.activation(act_hi[:], ps[1][:], ACT.Relu).then_inc(L.hi_ready, 1)

                def x_body(v, j):
                    act.wait_ge(L.x_e_ready, v + 1)
                    act.activation(x_weight[:], x_e[:], ACT.Exp, bias=x_small[:, 2:3])
                    act.drain()
                    by_head(x_msg, P, x_h, x_weight)
                    act.drain().then_inc(L.x_msg_ready, 1)

                def copy_out(t, half):
                    if t is None or n == 1:
                        return
                    act.wait_ge((L.first_done, L.second_done)[half], t.n + 1)
                    if half == 0 and not t.early(2):
                        act.wait_ge(L.stored[t.s], 16 * t.h)
                    act.activation(result[:, t.s, half * 512:half * 512 + 512], ps[0][:, half * 512:half * 512 + 512], ACT.Copy).then_inc(L.copied, 1)

                def messages(t):
                    if t is None:
                        return
                    act.wait_ge(L.e_ready, t.n + 1)
                    act.wait_ge(L.h_got[t.s], 32 * (t.h + 1))
                    if not t.early(1):
                        act.wait_ge(L.summed, t.n)
                    act.activation(weight_own[:, t.s, :], e_own[:, t.s, :], ACT.Exp)
                    for c in range(2):
                        act.activation(weight[:, c, :], e_in[:, c, :], ACT.Exp, bias=drop[:, t.s, c:c + 1])
                    act.drain()
                    act.activation(weight_own[:, t.s, :], weight_own[:, t.s, :], ACT.Copy, scale=self_count[:, bass.ds(t.n, 1)])
                    by_head(message[0], C0, near_h[0][:, t.s, :], weight[:, 0, :])
                    by_head(message[1], C1, near_h[1][:, t.s, :], weight[:, 1, :])
                    act.drain().then_inc(L.msg_ready, 1)

                def gate_input(t):
                    if t is None or n == 0:
                        return
                    act.wait_ge(xn2_turned, t.n + 1)
                    if not t.early(1):
                        act.wait_ge(gates_done, t.n)
                    act.activation(xT[:], ps[0][:, 512:1024], ACT.Copy).then_inc(xT_ready, 1)

                def step(s):
                    high(s(0))
                    if s(1) is not None:
                        more_chunks(act, s(1), x_body)
                    copy_out(s(-1), 1)
                    copy_out(s(0), 0)
                    gate_input(s(-2))
                    messages(s(2))
                steps(act, step, 2, 2)
                act.drain().then_inc(phase, 1)
                act.wait_ge(phase, 10 + 5 * n)
            gat_layer(0, layers[0])
            gat_layer(1, layers[1])
            act.wait_ge(consts, 3)
            act.wait_ge(to_log, 1)
            act.activation(logp[:], work[:], ACT.Ln).then_inc(from_log, 1)

            def split(e):
                act.wait_ge(ew_got[e % 2], 16 * (e // 2 + 1))
                act.activation(ew_hi[:, e, :, :], ew_in[:, e % 2, :, :], ACT.Copy).then_inc(ew_hi_done, 1)

            for i in range(SINKHORN_ITERS):
                act.wait_ge(to_log, 3 * i + 2)
                act.activation(work[:], work[:], ACT.Exp).then_inc(from_log, 1)
                act.wait_ge(share_done, 3 * i + 3)
                act.activation(col_b[:], ps[3][:, 520:528], ACT.Ln).then_inc(from_log, 1)
                if i < EXPERTS:
                    split(i)
                act.wait_ge(to_log, 3 * i + 3)
                act.activation(work[:], work[:], ACT.Exp).then_inc(from_log, 1)
                act.wait_ge(to_log, 3 * i + 4)
                act.activation(row_b[:], row_b[:], ACT.Ln).then_inc(from_log, 1)
            for e in range(SINKHORN_ITERS, EXPERTS):
                split(e)
            act.wait_ge(to_log, 3 * SINKHORN_ITERS + 2)
            act.activation(prob[:], logp[:], ACT.Exp).then_inc(from_log, 1)

            def high(t):
                if t is None:
                    return
                act.wait_ge(tok_turned, t.n + 1)
                if not t.early(2):
                    act.wait_ge(tok_done, t.n - 1)
                act.activation(tT_hi[:, t.s, :], ps[1][:, t.s * 512:t.s * 512 + 512], ACT.Copy).then_inc(tok_hi, 1)

            def scale(t):
                if t is None:
                    return
                act.wait_ge(tok_done, t.n + 1)
                if t.early(1):
                    act.wait_ge(lists_ready, 1)
                    act.wait_ge(ew_lo_done, EXPERTS)
                if not t.early(2):
                    act.wait_ge(added, 16 * (t.n - 1))
                act.activation(y_tok[:, t.s, :], ps[2 * t.s][:, 0:512], ACT.Copy, scale=factor[:, bass.ds(t.n, 1), :].rearrange("p o w -> p (o w)")).then_inc(y_ready, 1)

            def step(s):
                scale(s(-1))
                high(s(1))
            steps(act, step, 1, 1, NB)

        @block.tensor
        def _(pe):
            pe.wait_ge(consts, 1)
            pe.wait_ge(parts_ready, 1)
            pe.matmul(ps[3][:, 512:513], before[:], before_me[:], start=True, stop=True).then_inc(parts_summed, 1)
            pe.matmul(ps[3][:, 0:2 * TT], zero_b[:, 0:P], zero_b[:], start=True, stop=False)

            def transposes(t):
                if t is None:
                    return
                pe.wait_ge(xn_ready, t.n + 1)
                if not t.early(2):
                    pe.wait_ge(xlo_ready, t.n - 1)
                for k in range(KD):
                    mm = pe.transpose(ps[1][:, t.s * 512 + k * P:t.s * 512 + (k + 1) * P], x_norm[:, t.s, k * P:(k + 1) * P], ident[:])
                mm.then_inc(xt_ready, 1)

            def counts(t):
                if t is None:
                    return
                pe.wait_ge(hot_ready, t.n + 1)
                for u in range(2):
                    mm = pe.matmul(ps[3][:, 0:2 * TT], hot_lo[:, 2 * t.s + u, :], hot_hi[:, 2 * t.s + u, :], start=False, stop=False)
                mm.then_inc(hot_used, 1)

            def products(t):
                if t is None:
                    return
                pe.wait_ge(xlo_ready, t.n + 1)
                if not t.early(2):
                    pe.wait_ge(h1_left, t.n - 1)
                    pe.wait_ge(h1_right, t.n - 1)
                if t.early(1):
                    pe.wait_ge(w_lo_done, 2)
                    pe.wait_ge(w_hi_done, 2)
                o = ps[2 * t.s]
                for half in range(2):
                    for k in range(KD):
                        w = slice(k * H + half * 512, k * H + half * 512 + 512)
                        a = slice(k * P, (k + 1) * P)
                        cols = o[:, half * 512:half * 512 + 512]
                        pe.matmul(cols, xT_hi[:, t.s, a], wA_hi[:, w], start=(k == 0), stop=False)
                        pe.matmul(cols, xT_hi[:, t.s, a], wA_lo[:, w], start=False, stop=False)
                        pe.matmul(cols, xT_lo[:, t.s, a], wA_hi[:, w], start=False, stop=(k == KD - 1))
                cols = ps[3][:, 512:520]
                if not t.early(1):
                    pe.wait_ge(h1_right, t.n)
                for k in range(KD):
                    a = slice(k * P, (k + 1) * P)
                    pe.matmul(cols, xT_hi[:, t.s, a], wa_hi[0][:, k, :], start=(k == 0), stop=False)
                    pe.matmul(cols, xT_hi[:, t.s, a], wa_lo[0][:, k, :], start=False, stop=False)
                    mm = pe.matmul(cols, xT_lo[:, t.s, a], wa_hi[0][:, k, :], start=False, stop=(k == KD - 1))
                mm.then_inc(h1_ready, 1)

            def step(s):
                transposes(s(1))
                counts(s(0))
                products(s(0))
            steps(pe, step, 1)
            pe.matmul(ps[3][:, 0:2 * TT], zero_b[:, 0:P], zero_b[:], start=False, stop=True).then_inc(counts_done, 1)
            pe.wait_ge(parts_ready, 2)
            pe.matmul(ps[3][:, 512:512 + TT], ones[:], other_count[:], start=True, stop=True).then_inc(parts_summed, 1)
            pe.drain().then_inc(phase, 1)
            pe.wait_ge(phase, 5)
            pe.wait_ge(consts, 2)
            pe.wait_ge(fc_hi, 4)
            pe.wait_ge(fc_lo, 4)

            def gat_layer(n, L):
                w_hi, w_lo = ((wB_hi, wB_lo), (wA_hi, wA_lo))[n]
                width = (H, D)[n]
                pe.sem_inc(L.x_used, 1)

                def turn(t):
                    if t is None:
                        return
                    pe.wait_ge(L.gathered_ready, t.n + 1)
                    if not t.early(1):
                        pe.wait_ge(L.lo_ready, t.n)
                    for k in range(KH):
                        mm = pe.transpose(ps[1][:, k * P:(k + 1) * P], gathered[:, k * P:(k + 1) * P], ident[:])
                    mm.then_inc(L.turned, 1)

                def add(rows, one_hot, msg, w, start, stop):
                    for half in range(2):
                        pe.matmul(ps[2][:, half * 512:half * 512 + 512], one_hot, msg[0:rows, half * 512:half * 512 + 512], start=start, stop=stop)
                    return pe.matmul(ps[3][:, 512:512 + HEADS], one_hot, w, start=start, stop=stop)

                def sums(t):
                    if t is None:
                        return
                    pe.wait_ge(L.msg_ready, t.n + 1)
                    if not t.early(1):
                        pe.wait_ge(L.gathered_ready, t.n)
                    if not t.early(2):
                        if n == 0:
                            pe.wait_ge(L.extra_read, t.n - 1)
                        elif not t.early(4):
                            pe.wait_ge(L.extra_read, t.n - 3)
                    add(C0, hot[:, t.s, :], message[0], weight[:, 0, :], True, False)

                    def x_body(v, j):
                        pe.wait_ge(L.x_src_ready, v + 1)
                        pe.matmul(ps[3][:, 0:2 * HEADS], x_hot_t[:], maxima[:], start=True, stop=True).then_inc(L.x_at_edges, 1)
                        pe.wait_ge(L.x_msg_ready, v + 1)
                        add(P, x_hot[:], x_msg, x_weight[:], False, False).then_inc(L.x_used, 1)
                    more_chunks(pe, t, x_body)
                    add(C1, hot1[0:C1, t.s, :], message[1], weight[0:C1, 1, :], False, True).then_inc(L.summed, 1)

                def spread(t, before_t):
                    if t is None:
                        return
                    pe.wait_ge(L.diag_ready, t.n + 1)
                    if not t.early(1):
                        pe.wait_ge(L.denom_read, t.n)
                    pe.matmul(ps[3][:, 0:512], ones[:], diag[0][:].rearrange("p h e -> p (h e)"), start=True, stop=True)
                    pe.matmul(ps[3][:, 640:640 + HEADS * C1], ones[0:C1, :], diag[1][0:C1, :, :].rearrange("p h e -> p (h e)"),
                              start=True, stop=True).then_inc(L.spread, 1)

                    def m_body(v, j):
                        pe.wait_ge(L.m_diag_ready, v + 1)
                        pe.matmul(ps[3][:, 0:512], ones[:], m_diag[:].rearrange("p h e -> p (h e)"), start=True, stop=True).then_inc(L.m_spread, 1)
                    more_chunks(pe, t, m_body)

                def at_edges(t):
                    if t is None:
                        return
                    pe.wait_ge(L.max_ready, t.n + 1)
                    for c in range(2):
                        mm = pe.matmul(ps[3][:, 520 + 8 * c:528 + 8 * c], hot_t[:, c * P:(c + 1) * P], maxima[:], start=True, stop=True)
                    mm.then_inc(L.at_edges, 1)

                def product(t, part, after):
                    if t is None:
                        return
                    if part == 0:
                        pe.wait_ge(L.lo_ready, t.n + 1)
                        if not t.early(1):
                            pe.wait_ge(L.copied, 2 * t.n if n == 0 else t.n)
                    blocks = range(KH) if n == 0 else range(part * KH // 2, (part + 1) * KH // 2)
                    half = part if n == 0 else 0
                    cols = ps[0][:, half * 512:half * 512 + 512]
                    for k in blocks:
                        a = slice(k * P, (k + 1) * P)
                        w = slice(k * width + half * 512, k * width + half * 512 + 512)
                        pe.matmul(cols, act_hi[:, a], w_hi[:, w], start=(k == 0), stop=False)
                        pe.matmul(cols, act_hi[:, a], w_lo[:, w], start=False, stop=False)
                        mm = pe.matmul(cols, act_lo[:, a], w_hi[:, w], start=False, stop=(k == KH - 1))
                    if n == 0 and part == 1:
                        if after is not None:
                            pe.wait_ge(L.e_ready, after.n + 1)
                        else:
                            pe.wait_ge(L.denom_read, NT)
                        for k in range(KH):
                            a = slice(k * P, (k + 1) * P)
                            pe.matmul(ps[3][:, 536:544], act_hi[:, a], wa_hi[1][:, k, :], start=(k == 0), stop=False)
                            pe.matmul(ps[3][:, 536:544], act_hi[:, a], wa_lo[1][:, k, :], start=False, stop=False)
                            mm = pe.matmul(ps[3][:, 536:544], act_lo[:, a], wa_hi[1][:, k, :], start=False, stop=(k == KH - 1))
                    mm.then_inc((L.first_done, L.second_done)[part], 1)

                def gate_turn(t):
                    if t is None or n == 0:
                        return
                    pe.wait_ge(xn2_ready, t.n + 1)
                    if not t.early(1):
                        pe.wait_ge(xT_ready, t.n)
                    for k in range(KD):
                        mm = pe.transpose(ps[0][:, 512 + k * P:512 + (k + 1) * P], result[:, t.s, D + k * P:D + (k + 1) * P], ident[:])
                    mm.then_inc(xn2_turned, 1)

                def gate_product(t, after):
                    if t is None or n == 0:
                        return
                    pe.wait_ge(xT_ready, t.n + 1)
                    if after is not None:
                        pe.wait_ge(L.e_ready, after.n + 1)
                    else:
                        pe.wait_ge(L.denom_read, NT)
                    if not t.early(1):
                        pe.wait_ge(L.extra_read, t.n)
                    for k in range(KD):
                        mm = pe.matmul(ps[3][:, 544:552], xT[:, k * P:(k + 1) * P], gate_cols[:, k, :], start=(k == 0), stop=(k == KD - 1))
                    mm.then_inc(gates_done, 1)

                def step(s):
                    turn(s(0))
                    sums(s(1))
                    spread(s(2), s(1))
                    product(s(0), 0, None)
                    at_edges(s(2))
                    product(s(0), 1, s(2))
                    gate_turn(s(-1))
                    gate_product(s(-2), s(2))
                steps(pe, step, 2, 2)
                pe.drain().then_inc(phase, 1)
                pe.wait_ge(phase, 10 + 5 * n)
            gat_layer(0, layers[0])
            gat_layer(1, layers[1])
            for i in range(SINKHORN_ITERS):
                pe.wait_ge(share_ready, 3 * i + 1)
                pe.transpose(ps[3][0:EXPERTS, 0:P], col_a[:], ident[:]).then_inc(share_done, 1)
                pe.wait_ge(share_ready, 3 * i + 2)
                pe.matmul(ps[3][:, 512:520], ones[0:EXPERTS, :], col_diag[:], start=True, stop=True).then_inc(share_done, 1)
                pe.wait_ge(share_ready, 3 * i + 3)
                pe.matmul(ps[3][:, 520:528], ones[:], col_c[:], start=True, stop=True).then_inc(share_done, 1)
            with pe.Fori(0, FLOAT_BITS) as i:
                pe.wait_ge(share_ready, i + 3 * SINKHORN_ITERS + 1)
                pe.matmul(ps[3][:, 512:520], ones[:], col_a[:], start=True, stop=True).then_inc(share_done, 1)
            pe.wait_ge(share_ready, 3 * SINKHORN_ITERS + FLOAT_BITS + 1)
            for marks, within, whole in ((above_b, ps[0], ps[1]), (tie_b, ps[2], ps[3])):
                flat = marks[:].rearrange("p t e -> p (t e)")
                for a, b in ((0, 512), (512, NT * EXPERTS)):
                    pe.matmul(within[:, a:b], before_b[:], flat[:, a:b], start=True, stop=True)
                    mm = pe.matmul(whole[:, a:b], ones_b[:], flat[:, a:b], start=True, stop=True)
                mm.then_inc(share_done, 1)

            entries = ps[3][:, 0:EXPERTS * 3 * BLOCKS]
            width = 3 * BLOCKS

            def tile_entries(t):
                if t is None:
                    return
                pe.wait_ge(hots_ready, t.n + 1)
                if t.early(1):
                    pe.matmul(entries, zero_rb[:, 0:P], zero_rb[:], start=True, stop=False)
                for e in range(EXPERTS):
                    mm = pe.matmul(entries[:, e * width:(e + 1) * width], place_hot[:, t.s, e, :],
                                   block_val[:, t.s, e, :, :].rearrange("p v b -> p (v b)"), start=False, stop=False)
                mm.then_inc(hots_used, 1)

            def step(s):
                tile_entries(s(0))
            steps(pe, step, 0)
            pe.matmul(entries, zero_rb[:, 0:P], zero_rb[:], start=False, stop=True).then_inc(share_done, 1)
            pe.wait_ge(ew_hi_done, EXPERTS)
            pe.wait_ge(ew_lo_done, EXPERTS)

            def turn(t):
                if t is None:
                    return
                pe.wait_ge(tok_got[t.s], 16 * (t.h + 1))
                if not t.early(2):
                    pe.wait_ge(tok_lo, t.n - 1)
                for k in range(KD):
                    mm = pe.transpose(ps[1][:, t.s * 512 + k * P:t.s * 512 + (k + 1) * P], x_tok[:, t.s, k * P:(k + 1) * P], ident[:])
                mm.then_inc(tok_turned, 1)

            def product(t):
                if t is None:
                    return
                expert = pe.value_load(expert_of[0:1, bass.ds(t.n, 1)], min_val=0, max_val=EXPERTS - 1)
                pe.wait_ge(tok_lo, t.n + 1)
                if not t.early(2):
                    pe.wait_ge(y_ready, t.n - 1)
                cols = ps[2 * t.s][:, 0:512]
                for k in range(KD):
                    a = slice(k * P, (k + 1) * P)
                    hi, lo = (w[:, bass.ds(expert, 1), k, :].rearrange("p o n -> p (o n)") for w in (ew_hi, ew_lo))
                    pe.matmul(cols, tT_hi[:, t.s, a], hi, start=(k == 0), stop=False)
                    pe.matmul(cols, tT_hi[:, t.s, a], lo, start=False, stop=False)
                    mm = pe.matmul(cols, tT_lo[:, t.s, a], hi, start=False, stop=(k == KD - 1))
                mm.then_inc(tok_done, 1)

            def step(s):
                turn(s(1))
                product(s(0))
            steps(pe, step, 1, 0, NB)

        @block.vector
        def _(dve):
            dve.wait_ge(edges_in, 64)
            dve.wait_ge(consts, 1)
            dve.tensor_tensor(e_other[:], e_src[:], e_dst[:], ALU.not_equal)
            dve.tensor_copy(e_row[:, :, 0], e_src[:])
            dve.tensor_copy(e_row[:].bitcast(F32)[:, :, 1], e_dst[:])
            dve.tensor_scalar(e_tmp[:], e_dst[:], 7, None, ALU.logical_shift_right)
            dve.drain()
            dve.tensor_copy(e_hi[:], e_tmp[:])
            dve.tensor_tensor_scan(e_count[:], e_other[:], zeros_e[:], 0.0, ALU.add, ALU.add)
            dve.tensor_scalar(e_self[:], e_other[:], -1.0, 1.0, ALU.mult, ALU.add)
            dve.drain()
            dve.tensor_scalar(e_tmp[:], e_dst[:], P - 1, None, ALU.bitwise_and)
            dve.tensor_copy(before_me[:], e_count[:, EC - 1:EC]).then_inc(parts_ready, 1)
            dve.drain()
            dve.tensor_copy(e_lo[:], e_tmp[:])
            dve.tensor_tensor(e_count[:], e_count[:], e_other[:], ALU.subtract)
            dve.drain()
            dve.scalar_tensor_tensor(e_count[:], e_self[:], float(NOWHERE), e_count[:], ALU.mult, ALU.add)
            dve.drain()
            dve.wait_ge(parts_summed, 1)
            dve.tensor_scalar(e_pos[:], e_count[:], ps[3][:, 512:513], None, ALU.add)
            dve.drain().then_inc(rows_ready, 1)

            for n, (w, layer, piece) in enumerate(W_PIECES):
                hi, lo = ((wA_hi, wA_lo), (wB_hi, wB_lo))[layer]
                cols = slice(piece * 2048, (piece + 1) * 2048)
                dve.wait_ge(w_in[n % 2], 16 * (n // 2 + 1))
                dve.wait_ge(att_in[layer], 32)
                for m in range(2):
                    row = att_vec[:, m, :].rearrange("p (o n) -> p o n", o=1).to_broadcast((P, 2, H))
                    dve.tensor_tensor(prod[:].rearrange("p (k n) -> p k n", k=2), stage[:, n % 2, :].rearrange("p (k n) -> p k n", k=2), row, ALU.mult)
                    dve.drain()
                    dve.tensor_reduce(wa_f[:, 2 * piece:2 * piece + 2, m * HEADS:(m + 1) * HEADS],
                                      prod[:].rearrange("p (k h c) -> p k h c", k=2, h=HEADS), AX, ALU.add)
                    dve.drain()
                dve.tensor_copy(wa_hi[layer][:, 2 * piece:2 * piece + 2, :], wa_f[:, 2 * piece:2 * piece + 2, :])
                dve.drain()
                dve.tensor_tensor(wa_lo[layer][:, 2 * piece:2 * piece + 2, :], wa_f[:, 2 * piece:2 * piece + 2, :],
                                  wa_hi[layer][:, 2 * piece:2 * piece + 2, :].bitcast(F32), ALU.subtract)
                dve.wait_ge(w_hi_done, n + 1)
                dve.tensor_tensor(lo[:, cols], stage[:, n % 2, :], hi[:, cols].bitcast(F32), ALU.subtract)
                dve.drain().then_inc(w_lo_done, 1)

            def statistics(t):
                if t is None:
                    return
                dve.wait_ge(x_got[t.s], 16 * (t.h + 1))
                dve.bn_stats(ln_stats[:, t.s, :], x_in[:, t.s, :])
                dve.drain()
                dve.bn_aggr(ln_mv[:, t.s, :], ln_stats[:, t.s, :]).then_inc(mv_ready, 1)

            def one_hots(t):
                if t is None:
                    return
                if not t.early(2):
                    dve.wait_ge(hot_used, t.n - 1)
                for u in range(2):
                    j, slot = bass.ds(2 * t.n + u, 1), 2 * t.s + u
                    dve.tensor_scalar(hot_lo[:, slot, :], iota[:], e_lo[:, j], None, ALU.is_equal)
                    dve.tensor_scalar(hot_hi[:, slot, 0:TT], iota[:, 0:TT], e_hi[:, j], e_self[:, j], ALU.is_equal, ALU.mult)
                    dve.tensor_scalar(hot_hi[:, slot, TT:2 * TT], iota[:, 0:TT], e_hi[:, j], e_other[:, j], ALU.is_equal, ALU.mult)
                dve.drain().then_inc(hot_ready, 1)

            def normalise(t):
                if t is None:
                    return
                dve.wait_ge(std_ready, t.n + 1)
                dve.reciprocal(ln_rstd[:, t.s, :], ln_std[:, t.s, :])
                dve.drain()
                dve.scalar_tensor_tensor(ln_step[:, t.s, :], ln_mv[:, t.s, 1:2], EPS_LN, ln_rstd[:, t.s, :], ALU.add, ALU.mult)
                dve.drain()
                dve.tensor_tensor(ln_step[:, t.s, :], ln_step[:, t.s, :], ln_rstd[:, t.s, :], ALU.mult)
                dve.drain()
                dve.tensor_scalar(ln_step[:, t.s, :], ln_step[:, t.s, :], -0.5, 1.5, ALU.mult, ALU.add)
                dve.drain()
                dve.tensor_tensor(ln_rstd[:, t.s, :], ln_rstd[:, t.s, :], ln_step[:, t.s, :], ALU.mult)
                dve.drain()
                if not t.early(2):
                    dve.wait_ge(xt_ready, t.n - 1)
                dve.tensor_scalar(x_norm[:, t.s, :], x_in[:, t.s, :], ln_mv[:, t.s, 0:1], ln_rstd[:, t.s, 0:1],
                                  ALU.subtract, ALU.mult).then_inc(xn_ready, 1)

            def low(t):
                if t is None:
                    return
                dve.wait_ge(xhi_ready, t.n + 1)
                dve.tensor_tensor(xT_lo[:, t.s, :], ps[1][:, t.s * 512:t.s * 512 + 512], xT_hi[:, t.s, :].bitcast(F32),
                                  ALU.subtract).then_inc(xlo_ready, 1)

            def right(t):
                if t is None:
                    return
                dve.wait_ge(h1_ready, t.n + 1)
                if not t.early(2):
                    dve.wait_ge(h1_stored[t.s], 16 * t.h)
                dve.tensor_copy(h_out[:, t.s, 512:H], ps[2 * t.s][:, 512:H])
                dve.tensor_copy(att[0][:, bass.ds(t.n, 1), :].rearrange("p o a -> p (o a)"), ps[3][:, 512:520])
                dve.drain().then_inc(h1_right, 1)

            def step(s):
                right(s(-1))
                one_hots(s(1))
                statistics(s(2))
                low(s(1))
                normalise(s(2))
            steps(dve, step, 2, 1)

            dve.wait_ge(counts_done, 1)
            dve.tensor_scalar(self_count[:], ps[3][:, 0:TT], 1.0, None, ALU.add)
            dve.tensor_copy(other_count[:], ps[3][:, TT:2 * TT])
            dve.drain().then_inc(parts_ready, 1)
            dve.wait_ge(parts_summed, 2)
            dve.tensor_copy(tile_sum[:], ps[3][:, 512:512 + TT])
            dve.drain()
            dve.tensor_tensor_scan(tile_scan[:], tile_sum[:], zeros_e[:, 0:TT], 0.0, ALU.add, ALU.add)
            dve.tensor_scalar(loops_i[:], tile_sum[0:1, :], float(P - 1 - C0 - C1), 0.0, ALU.add, ALU.max)
            dve.drain()
            dve.tensor_tensor(table[:, 0, :], tile_scan[0:1, :], tile_sum[0:1, :], ALU.subtract)
            dve.tensor_scalar(table[:, 1, :], loops_i[:], 7, None, ALU.logical_shift_right)
            dve.drain()
            dve.tensor_copy(loops_f[:], table[:, 1, :])
            dve.drain()
            dve.tensor_tensor_scan(loops_scan[:], loops_f[:], zeros_e[0:1, 0:TT], 0.0, ALU.add, ALU.add)
            dve.drain()
            dve.tensor_tensor(table[:, 2, :], loops_scan[:], loops_f[:], ALU.subtract)
            dve.drain().then_inc(table_done, 1)
            dve.drain().then_inc(phase, 1)
            dve.wait_ge(phase, 5)
            for n in range(4):
                dve.wait_ge(fc_hi, n + 1)
                dve.tensor_tensor(wA_lo[:, n * 1024:(n + 1) * 1024], own[:, n % 2, :], wA_hi[:, n * 1024:(n + 1) * 1024].bitcast(F32), ALU.subtract).then_inc(fc_lo, 1)
            dve.wait_ge(small_in, 32)
            dve.wait_ge(consts, 2)

            def gat_layer(n, L):
                dve.sem_inc(L.m_used, 1)
                dve.wait_ge(bias_in, 16 * (n + 1))

                def low(t):
                    if t is None:
                        return
                    dve.wait_ge(L.hi_ready, t.n + 1)
                    dve.scalar_tensor_tensor(act_lo[:], ps[1][:], 0.0, act_hi[:].bitcast(F32), ALU.max, ALU.subtract).then_inc(L.lo_ready, 1)

                def leaky(to, a):
                    dve.scalar_tensor_tensor(to, a, SLOPE, a, ALU.mult, ALU.max)

                def sources(t):
                    if t is None:
                        return
                    dve.wait_ge(L.listed[t.s], 32 * (t.h + 1))
                    dve.tensor_scalar(at_tile[:, t.s, :], ix[:, t.s, :, :].bitcast(F32)[:, :, 1], tile_base[:, bass.ds(t.n, 1)], None, ALU.subtract)
                    dve.drain()
                    dve.tensor_scalar(off_tile[:, t.s, :], at_tile[:, t.s, :], float(P), float(NOWHERE), ALU.is_ge, ALU.mult)
                    dve.tensor_scalar(drop[:, t.s, :], at_tile[:, t.s, :], float(P), -BIG, ALU.is_ge, ALU.mult)
                    dve.drain()
                    dve.tensor_tensor(src_ok[:, t.s, :, :].rearrange("p c o -> p (c o)"), ix[:, t.s, :, 0], off_tile[:, t.s, :], ALU.add).then_inc(L.src_ready, 1)

                def masks(t):
                    if t is None:
                        return
                    dve.tensor_scalar(hot[:, t.s, :], iota[:], at_tile[:, t.s, 0:1], None, ALU.is_equal)
                    dve.tensor_scalar(hot1[0:C1, t.s, :], iota[0:C1, :], at_tile[0:C1, t.s, 1:2], None, ALU.is_equal)
                    dve.tensor_scalar(hot_t[:, 0:C0 + C1], dst_row[:, t.s, :, :].bitcast(F32)[:, :, 1], node_id[:, bass.ds(t.n, 1)], None, ALU.is_equal)
                    dve.drain()
                    dve.tensor_scalar(miss[:], hot_t[:, 0:C0 + C1], 1.0, BIG, ALU.subtract, ALU.mult)
                    dve.drain()

                def highest(t):
                    if t is None:
                        return
                    dve.wait_ge(L.spread, t.n + 1)
                    for a, b, bank in ((0, C0, ps[3][:, 0:512]), (C0, C0 + C1, ps[3][:, 640:640 + HEADS * C1])):
                        dve.tensor_tensor(seen[:, :, a:b], bank.rearrange("p (h e) -> p h e", h=HEADS),
                                          miss[:, a:b].rearrange("p (o e) -> p o e", o=1).to_broadcast((P, HEADS, b - a)), ALU.add)
                    dve.drain()
                    dve.tensor_reduce(top[:], seen[:], AX, ALU.max)
                    dve.drain()
                    mine = att[n][:, bass.ds(t.n, 1), :].rearrange("p o a -> p (o a)")
                    dve.tensor_tensor(top[:], top[:], mine[:, 0:HEADS], ALU.max)
                    dve.drain()

                    def m_body(v, j):
                        dve.wait_ge(L.m_listed, 32 * (v + 1))
                        dve.tensor_scalar(m_small[:, 0:1], m_ix[:].bitcast(F32)[:, 1:2], tile_base[:, bass.ds(t.n, 1)], None, ALU.subtract)
                        dve.tensor_scalar(m_miss[:], m_row[:].bitcast(F32)[:, :, 1], node_id[:, bass.ds(t.n, 1)], None, ALU.is_equal)
                        dve.drain()
                        dve.tensor_scalar(m_small[:, 1:2], m_small[:, 0:1], float(P), float(NOWHERE), ALU.is_ge, ALU.mult)
                        dve.tensor_scalar(m_miss[:], m_miss[:], 1.0, BIG, ALU.subtract, ALU.mult)
                        dve.drain()
                        dve.tensor_tensor(m_src[:], m_ix[:, 0:1], m_small[:, 1:2], ALU.add).then_inc(L.m_src_ready, 1)
                        dve.wait_ge(L.m_spread, v + 1)
                        dve.tensor_tensor(seen[:, :, 0:P], ps[3][:, 0:512].rearrange("p (h e) -> p h e", h=HEADS),
                                          m_miss[:].rearrange("p (o e) -> p o e", o=1).to_broadcast((P, HEADS, P)), ALU.add)
                        dve.drain()
                        dve.tensor_reduce(m_top[:], seen[:, :, 0:P], AX, ALU.max)
                        dve.drain()
                        dve.tensor_tensor(top[:], top[:], m_top[:], ALU.max)
                        dve.drain().then_inc(L.m_used, 1)
                    more_chunks(dve, t, m_body)

                    dve.tensor_tensor(e_own[:, t.s, :], mine[:, 0:HEADS], mine[:, HEADS:2 * HEADS], ALU.add)
                    dve.tensor_tensor(top[:], top[:], mine[:, HEADS:2 * HEADS], ALU.add)
                    dve.tensor_copy(maxima[:, HEADS:2 * HEADS], mine[:, HEADS:2 * HEADS])
                    dve.drain()
                    leaky(maxima[:, 0:HEADS], top[:])
                    leaky(e_own[:, t.s, :], e_own[:, t.s, :])
                    dve.drain()
                    dve.tensor_tensor(e_own[:, t.s, :], e_own[:, t.s, :], maxima[:, 0:HEADS], ALU.subtract)
                    dve.drain().then_inc(L.max_ready, 1)

                def exponents(t):
                    if t is None:
                        return
                    dve.wait_ge(L.at_edges, t.n + 1)
                    if not t.early(1):
                        dve.wait_ge(L.msg_ready, t.n)
                    at = ps[3][:, 520:536].rearrange("p (c a) -> p c a", c=2)
                    dve.tensor_tensor(e_in[:], near_att[:, t.s, :, 0:HEADS], at[:, :, HEADS:2 * HEADS], ALU.add)
                    dve.drain()
                    leaky(e_in[:], e_in[:])
                    dve.drain()
                    dve.tensor_tensor(e_in[:], e_in[:], at[:, :, 0:HEADS], ALU.subtract).then_inc(L.e_ready, 1)

                def x_body_of(t):
                    def x_body(v, j):
                        dve.wait_ge(L.x_listed, 32 * (v + 1))
                        dve.tensor_scalar(x_small[:, 0:1], x_ix[:].bitcast(F32)[:, 1:2], tile_base[:, bass.ds(t.n, 1)], None, ALU.subtract)
                        dve.tensor_scalar(x_hot_t[:], x_row[:].bitcast(F32)[:, :, 1], node_id[:, bass.ds(t.n, 1)], None, ALU.is_equal)
                        dve.drain()
                        dve.tensor_scalar(x_hot[:], iota[:], x_small[:, 0:1], None, ALU.is_equal)
                        dve.tensor_scalar(x_small[:, 1:2], x_small[:, 0:1], float(P), float(NOWHERE), ALU.is_ge, ALU.mult)
                        dve.tensor_scalar(x_small[:, 2:3], x_small[:, 0:1], float(P), -BIG, ALU.is_ge, ALU.mult)
                        dve.drain()
                        dve.tensor_tensor(x_src[:], x_ix[:, 0:1], x_small[:, 1:2], ALU.add)
                        dve.drain().then_inc(L.x_src_ready, 1)
                        dve.wait_ge(L.x_at_edges, v + 1)
                        dve.wait_ge(L.x_got, 32 * (v + 1))
                        dve.tensor_tensor(x_e[:], x_att[:, 0:HEADS], ps[3][:, HEADS:2 * HEADS], ALU.add)
                        dve.drain()
                        leaky(x_e[:], x_e[:])
                        dve.drain()
                        dve.tensor_tensor(x_e[:], x_e[:], ps[3][:, 0:HEADS], ALU.subtract).then_inc(L.x_e_ready, 1)
                    return x_body

                def denominators(t):
                    if t is None:
                        return
                    dve.wait_ge(L.summed, t.n + 1)
                    dve.scalar_tensor_tensor(denom[:], ps[3][:, 512:512 + HEADS], 1e-16, weight_own[:, t.s, :], ALU.add, ALU.add).then_inc(L.denom_read, 1)

                def gather(t):
                    if t is None:
                        return
                    dve.drain()
                    dve.wait_ge(L.own_ready, t.n + 1)
                    dve.reciprocal(denom[:], denom[:])
                    dve.tensor_tensor(total[:], ps[2][:], own_msg[:], ALU.add)
                    dve.drain()
                    if not t.early(1):
                        dve.wait_ge(L.turned, t.n)
                    for m in range(HEADS):
                        c = slice(m * HID, (m + 1) * HID)
                        dve.scalar_tensor_tensor(gathered[:, c], total[:, c], denom[:, m:m + 1], bias_row[:, c], ALU.mult, ALU.add)
                    dve.drain().then_inc(L.gathered_ready, 1)

                def terms(t):
                    if t is None or n == 1:
                        return
                    dve.wait_ge(L.second_done, t.n + 1)
                    dve.tensor_copy(att[1][:, bass.ds(t.n, 1), :].rearrange("p o a -> p (o a)"), ps[3][:, 536:544]).then_inc(L.extra_read, 1)

                def gate_terms(t):
                    if t is None or n == 0:
                        return
                    dve.wait_ge(gates_done, t.n + 1)
                    dve.tensor_copy(gates[:, bass.ds(t.n, 1), :].rearrange("p o a -> p (o a)"), ps[3][:, 544:552]).then_inc(L.extra_read, 1)

                def residual(t):
                    if t is None or n == 0:
                        return
                    dve.wait_ge(L.second_done, t.n + 1)
                    dve.wait_ge(x_plus_ready, t.n + 1)
                    if not t.early(2):
                        dve.wait_ge(L.stored[t.s], 32 * t.h)
                        dve.wait_ge(xn2_turned, t.n - 1)
                    dve.tensor_tensor(result[:, t.s, 0:D], ps[0][:, 0:D], x_plus[:], ALU.add).then_inc(L.copied, 1)

                def moments(t):
                    if t is None or n == 0:
                        return
                    dve.drain()
                    dve.bn_stats(ln2[:, 0:6], result[:, t.s, 0:D])
                    dve.drain()
                    dve.bn_aggr(ln2[:, 6:8], ln2[:, 0:6])
                    dve.drain()
                    dve.tensor_scalar(ln2[:, 8:9], ln2[:, 7:8], EPS_LN, None, ALU.add).then_inc(var_ready, 1)

                def normalise2(t):
                    if t is None or n == 0:
                        return
                    dve.wait_ge(pow_ready, t.n + 1)
                    dve.tensor_tensor(ln2[:, 10:11], ln2[:, 9:10], ln2[:, 9:10], ALU.mult)
                    dve.drain()
                    dve.tensor_tensor(ln2[:, 10:11], ln2[:, 10:11], ln2[:, 8:9], ALU.mult)
                    dve.drain()
                    dve.tensor_scalar(ln2[:, 10:11], ln2[:, 10:11], -0.5, 1.5, ALU.mult, ALU.add)
                    dve.drain()
                    dve.tensor_tensor(ln2[:, 11:12], ln2[:, 9:10], ln2[:, 10:11], ALU.mult)
                    dve.drain()
                    dve.tensor_scalar(result[:, t.s, D:2 * D], result[:, t.s, 0:D], ln2[:, 6:7], ln2[:, 11:12], ALU.subtract, ALU.mult)
                    dve.drain().then_inc(xn2_ready, 1)

                def step(s):
                    terms(s(-1))
                    gate_terms(s(-3))
                    residual(s(-1))
                    low(s(0))
                    if s(1) is not None:
                        more_chunks(dve, s(1), x_body_of(s(1)))
                    denominators(s(1))
                    masks(s(2))
                    highest(s(2))
                    moments(s(-1))
                    gather(s(1))
                    normalise2(s(-1))
                    exponents(s(2))
                    sources(s(3))
                steps(dve, step, 3, 3)
                dve.drain().then_inc(phase, 1)
                dve.wait_ge(phase, 10 + 5 * n)
            gat_layer(0, layers[0])
            gat_layer(1, layers[1])
            dve.wait_ge(consts, 3)
            dve.tensor_scalar(work[:], gates[:], GATE_MIN, None, ALU.max)
            dve.drain().then_inc(to_log, 1)
            dve.wait_ge(from_log, 1)

            def by_token(a):
                return a.rearrange("p (t o) -> p t o", o=1).to_broadcast((P, NT, EXPERTS))

            def by_expert(a):
                return a.rearrange("p (o e) -> p o e", o=1).to_broadcast((P, NT, EXPERTS))

            def mask_outside():
                dve.drain()
                dve.tensor_scalar(logp[:, NT - 1, :], logp[:, NT - 1, :], outside_neg[:, 0:1], None, ALU.add)
                dve.drain()

            mask_outside()
            for i in range(SINKHORN_ITERS):
                dve.tensor_reduce(col_a[:], logp[:].rearrange("p t e -> p e t"), AX, ALU.max).then_inc(share_ready, 1)
                dve.wait_ge(share_done, 3 * i + 1)
                dve.tensor_reduce(col_t[:], ps[3][0:EXPERTS, 0:P], AX, ALU.max)
                dve.drain()
                dve.tensor_scalar(col_diag[:], ident[0:EXPERTS, 0:EXPERTS], col_t[:, 0:1], None, ALU.mult).then_inc(share_ready, 1)
                dve.wait_ge(share_done, 3 * i + 2)
                dve.tensor_copy(col_a[:], ps[3][:, 512:520])
                dve.drain()
                dve.tensor_tensor(work[:], logp[:], by_expert(col_a[:]), ALU.subtract).then_inc(to_log, 1)
                dve.wait_ge(from_log, 4 * i + 2)
                dve.tensor_reduce(col_c[:], work[:].rearrange("p t e -> p e t"), AX, ALU.add).then_inc(share_ready, 1)
                dve.wait_ge(from_log, 4 * i + 3)
                dve.tensor_tensor(col_a[:], col_a[:], col_b[:], ALU.add)
                dve.drain()
                dve.tensor_tensor(logp[:], logp[:], by_expert(col_a[:]), ALU.subtract)
                dve.drain()
                dve.tensor_reduce(row_a[:], logp[:], AX, ALU.max)
                dve.drain()
                dve.tensor_tensor(work[:], logp[:], by_token(row_a[:]), ALU.subtract).then_inc(to_log, 1)
                dve.wait_ge(from_log, 4 * i + 4)
                dve.tensor_reduce(row_b[:], work[:], AX, ALU.add).then_inc(to_log, 1)
                dve.wait_ge(from_log, 4 * i + 5)
                dve.tensor_tensor(row_a[:], row_a[:], row_b[:], ALU.add)
                dve.drain()
                dve.tensor_tensor(logp[:], logp[:], by_token(row_a[:]), ALU.subtract)
                if i < SINKHORN_ITERS - 1:
                    mask_outside()
            dve.drain().then_inc(to_log, 1)
            dve.wait_ge(from_log, 4 * SINKHORN_ITERS + 2)
            dve.tensor_scalar(prob[:, NT - 1, :], prob[:, NT - 1, :], inside[:, 0:1], outside[:, NT - 1:NT], ALU.mult, ALU.subtract)
            dve.drain()

            with dve.Fori(0, FLOAT_BITS) as i:
                dve.tensor_tensor(trial[:], found[:], bit[:], ALU.bitwise_or)
                dve.drain()
                dve.tensor_tensor(work[:], prob[:], by_expert(trial[:].bitcast(F32)), ALU.is_ge)
                dve.drain()
                dve.tensor_reduce(col_a[:], work[:].rearrange("p t e -> p e t"), AX, ALU.add).then_inc(share_ready, 1)
                dve.wait_ge(share_done, i + 3 * SINKHORN_ITERS + 1)
                dve.scalar_tensor_tensor(trial[:], ps[3][:, 512:520], float(TOPK), bit[:], ALU.is_ge, ALU.mult)
                dve.drain()
                dve.tensor_tensor(found[:], found[:], trial[:], ALU.bitwise_or)
                dve.tensor_scalar(bit[:], bit[:], 1, None, ALU.logical_shift_right)
                dve.drain()

            dve.tensor_tensor(above[:], prob[:], by_expert(found[:].bitcast(F32)), ALU.is_gt)
            dve.tensor_tensor(tie[:], prob[:], by_expert(found[:].bitcast(F32)), ALU.is_equal)
            dve.drain()
            dve.tensor_copy(above_b[:], above[:])
            dve.tensor_copy(tie_b[:], tie[:])
            dve.drain().then_inc(share_ready, 1)

            def ranks(within, whole):
                dve.tensor_copy(work[:].rearrange("p t e -> p (t e)"), whole[:, 0:NT * EXPERTS])
                dve.drain()
                for e in range(EXPERTS):
                    dve.tensor_tensor_scan(scan[:, :, e], work[:, :, e], zeros_r[:], 0.0, ALU.add, ALU.add)
                dve.drain()
                dve.tensor_tensor(work[:], scan[:], work[:], ALU.subtract)
                dve.tensor_copy(col_a[:], scan[:, NT - 1, :])
                dve.drain()
                dve.tensor_tensor(place[:].rearrange("p t e -> p (t e)"), within[:, 0:NT * EXPERTS], work[:].rearrange("p t e -> p (t e)"), ALU.add)
                dve.drain()

            dve.wait_ge(share_done, 3 * SINKHORN_ITERS + FLOAT_BITS + 2)
            ranks(ps[0], ps[1])
            dve.tensor_copy(col_b[:], col_a[:])
            dve.tensor_tensor(place_hi[:], place[:], above[:], ALU.mult)
            dve.drain()
            ranks(ps[2], ps[3])
            dve.tensor_scalar(col_c[:], col_b[:], -1.0, float(TOPK), ALU.mult, ALU.add)
            dve.drain()
            dve.tensor_tensor(work[:], place[:], by_expert(col_c[:]), ALU.is_lt)
            dve.tensor_tensor(place[:], place[:], by_expert(col_b[:]), ALU.add)
            dve.drain()
            dve.tensor_tensor(tie[:], tie[:], work[:], ALU.mult)
            dve.drain()
            dve.tensor_tensor(place[:], place[:], tie[:], ALU.mult)
            dve.tensor_tensor(above[:], above[:], tie[:], ALU.add)
            dve.drain()
            dve.tensor_tensor(place[:], place[:], place_hi[:], ALU.add)
            dve.tensor_scalar(work[:], above[:], -float(NOWHERE), float(NOWHERE), ALU.mult, ALU.add)
            dve.tensor_reduce(row_a[:], above[:], AX, ALU.add)
            dve.scalar_tensor_tensor(code[:], prob[:], 0.5, above[:], ALU.is_gt, ALU.mult)
            dve.drain()
            dve.tensor_tensor(place_i[:], place[:], work[:], ALU.add)
            dve.tensor_scalar(row_a[:], row_a[:], 1.0, None, ALU.add)
            dve.drain()
            dve.tensor_scalar(work[:].bitcast(I32), place_i[:], 7, None, ALU.logical_shift_right)
            dve.tensor_scalar(scan[:].bitcast(I32), place_i[:], P - 1, None, ALU.bitwise_and)
            dve.tensor_tensor(code[:], code[:], by_token(row_a[:]), ALU.mult)
            dve.drain()
            dve.tensor_copy(place_hi[:], work[:].bitcast(I32))
            dve.tensor_copy(place_lo[:], scan[:].bitcast(I32))
            dve.drain()

            def hots(t):
                if t is None:
                    return
                if not t.early(2):
                    dve.wait_ge(hots_used, t.n - 1)
                lo = place_lo[:, bass.ds(t.n, 1), :].rearrange("p o e -> p (e o)")
                hi = place_hi[:, bass.ds(t.n, 1), :].rearrange("p o e -> p (e o)")
                val = code[:, bass.ds(t.n, 1), :].rearrange("p o e -> p (e o)")

                def wide(a, n):
                    return a.rearrange("p (e o) -> p e o", o=1).to_broadcast((P, EXPERTS, n))
                dve.tensor_tensor(place_hot[:, t.s, :, :], iota[:].rearrange("p (o n) -> p o n", o=1).to_broadcast((P, EXPERTS, P)), wide(lo, P), ALU.is_equal)
                dve.tensor_tensor(block_hot[:, t.s, :, :], iota[:, 0:BLOCKS].rearrange("p (o n) -> p o n", o=1).to_broadcast((P, EXPERTS, BLOCKS)), wide(hi, BLOCKS), ALU.is_equal)
                dve.drain()
                dve.tensor_scalar(block_val[:, t.s, :, 0, :], block_hot[:, t.s, :, :], tile_no[:, bass.ds(t.n, 1)], None, ALU.mult)
                dve.tensor_scalar(block_val[:, t.s, :, 1, :], block_hot[:, t.s, :, :], node_id[:, 0:1], None, ALU.mult)
                dve.tensor_tensor(block_val[:, t.s, :, 2, :], block_hot[:, t.s, :, :], wide(val, BLOCKS), ALU.mult)
                dve.drain().then_inc(hots_ready, 1)

            def step(s):
                hots(s(0))
            steps(dve, step, 0)
            dve.wait_ge(share_done, 3 * SINKHORN_ITERS + FLOAT_BITS + 3)
            dve.tensor_copy(listed_f[:].rearrange("p e v b -> p (e v b)"), ps[3][:, 0:EXPERTS * 3 * BLOCKS])
            dve.drain()
            dve.scalar_tensor_tensor(token_f[:], listed_f[:, :, 0, :], float(P), listed_f[:, :, 1, :], ALU.mult, ALU.add)
            dve.tensor_scalar(place[:, 0:BLOCKS, :].rearrange("p b e -> p e b"), listed_f[:, :, 2, :], 1.0, None, ALU.max)
            dve.drain()
            dve.scalar_tensor_tensor(token_f[:, :, BLOCKS - 1], token_f[:, :, 0], past_end[:, 0:1], token_f[:, :, BLOCKS - 1], ALU.mult, ALU.add)
            dve.reciprocal(scan[:, 0:BLOCKS, :].rearrange("p b e -> p e b"), place[:, 0:BLOCKS, :].rearrange("p b e -> p e b"))
            dve.drain()
            dve.tensor_copy(token[:].rearrange("p (e b) o -> p e (b o)", e=EXPERTS), token_f[:])
            dve.scalar_tensor_tensor(factor[:].rearrange("p (e b) o -> p e (b o)", e=EXPERTS), listed_f[:, :, 2, :], 0.0,
                                     scan[:, 0:BLOCKS, :].rearrange("p b e -> p e b"), ALU.is_gt, ALU.mult)
            dve.drain().then_inc(lists_ready, 1)

            def fetch_index(t):
                if t is None:
                    return
                if not t.early(2):
                    dve.wait_ge(tok_got[t.s], 16 * t.h)
                dve.tensor_copy(fetch_at[:, t.s, :], token[:, bass.ds(t.n, 1), :].rearrange("p o w -> p (o w)")).then_inc(fetch_ready, 1)

            def add_index(t):
                if t is None:
                    return
                if not t.early(2):
                    dve.wait_ge(added, 16 * (t.n - 1))
                dve.tensor_copy(add_at[:, t.s, :], token[:, bass.ds(t.n, 1), :].rearrange("p o w -> p (o w)")).then_inc(add_ready, 1)

            def low(t):
                if t is None:
                    return
                dve.wait_ge(tok_hi, t.n + 1)
                dve.tensor_tensor(tT_lo[:, t.s, :], ps[1][:, t.s * 512:t.s * 512 + 512], tT_hi[:, t.s, :].bitcast(F32), ALU.subtract).then_inc(tok_lo, 1)

            def step(s):
                fetch_index(s(3))
                low(s(1))
                add_index(s(0))
            steps(dve, step, 3, 0, NB)


_INS = ['x', 'src', 'dst', 'L0_gnn_W1', 'L0_gnn_att_src1', 'L0_gnn_att_dst1', 'L0_gnn_b1', 'L0_gnn_W2', 'L0_gnn_att_src2',
        'L0_gnn_att_dst2', 'L0_gnn_b2', 'L0_gnn_fcW', 'L0_gnn_fcb', 'L0_ffn_gate_w', 'L0_ffn_experts']
_OUTS = [((N, D), 'float32')]


def kernel(**inputs):
    import numpy as _np
    import concourse.bacc as _bacc
    from concourse import mybir as _mybir
    from concourse.bass_utils import run_bass_kernel_spmd as _run

    nc = _bacc.Bacc("TRN2", target_bir_lowering=False, num_devices=1)
    arrays, args = {}, []
    for name in _INS:
        a = _np.ascontiguousarray(inputs[name])
        arrays[f"in_{name}_dram"] = a
        args.append(nc.dram_tensor(f"in_{name}_dram", a.shape, _mybir.dt.from_np(a.dtype), kind="ExternalInput").ap())
    for i, (shape, dtype) in enumerate(_OUTS):
        dt = _mybir.dt.from_np(_np.dtype(dtype))
        args.append(nc.dram_tensor(f"out_{i}_dram", shape, dt, kind="ExternalOutput").ap())
    gnn_ffn_kernel(nc, *args)
    r = _run(nc, [arrays], core_ids=[0])
    got = tuple(r.results[0][f"out_{i}_dram"] for i in range(len(_OUTS)))
    return got[0]
```

```python
from contextlib import ExitStack

import concourse.bass as bass
from concourse import mybir

F32 = mybir.dt.float32
F32R = mybir.dt.float32r
BF16 = mybir.dt.bfloat16
I32 = mybir.dt.int32
ALU = mybir.AluOpType
ACT = mybir.ActivationFunctionType
AX = mybir.AxisListType.X

P = 128
N = 10000
E = 20000
D = 512
HEADS, HID = 4, 256
H = HEADS * HID
KD, KH = D // P, H // P
NT = (N + P - 1) // P
LAST = N - (NT - 1) * P
NPAD = NT * P
TT = 84
EC = 158
EROWS, EREST = E // EC, E % EC
PACKED = P * EC + 4 * P
NOWHERE = 1 << 20
C0, C1 = 128, 32
SLOPE = 0.2
BIG = 1e30
EXPERTS = 8
TOPK = N // EXPERTS
BLOCKS = (TOPK + P - 1) // P
LAST_ROWS = TOPK - (BLOCKS - 1) * P
EPS_LN = 1e-5
SINKHORN_ITERS = 8
GATE_MIN = 1e-10
BITS = 6
FLOAT_BITS = 30


class Tile:

    def __init__(self, k, c):
        self.n = 2 * k + c
        self.h = k + c // 2
        self.s = c % 2

    def early(self, lag):
        return isinstance(self.n, int) and self.n < lag


def steps(eng, body, before, after=0, tiles=NT):
    def straight(i):
        def step(d):
            return Tile(i // 2, i % 2 + d) if 0 <= i + d < tiles else None
        body(step)

    lo, hi = 4, (tiles - 4) // 2 * 2
    for i in range(-before, lo):
        straight(i)
    with eng.Fori(lo // 2, hi // 2) as k:
        for c in range(2):
            body(lambda d, k=k, c=c: Tile(k, c + d))
    for i in range(hi, tiles + after):
        straight(i)


def gnn_ffn_kernel(nc, x, src, dst, W1, att_src1, att_dst1, b1, W2, att_src2, att_dst2, b2, fcW, fcb,
                   gate_w, experts, out):
    ctx = ExitStack()
    with ctx:
        def sb(name, shape, dt=F32):
            return ctx.enter_context(nc.sbuf_tensor(name, shape, dt))

        def sem(name):
            return ctx.enter_context(nc.semaphore(name))

        def dram(name, shape, dt=F32):
            return nc.dram_tensor(name, shape, dt, kind="Internal").ap()

        packed = dram("packed", (PACKED, 2), I32)
        h_rows = [dram(f"h_rows{n}", (NPAD, H)) for n in (1, 2)]
        xn_rows = dram("xn_rows", (N, D))
        att_rows = [dram(f"att_rows{n}", (NPAD, 2 * HEADS)) for n in (1, 2)]

        ps = [ctx.enter_context(nc.psum_tensor(f"ps{n}", [P, 1024], F32)) for n in range(4)]

        ident = sb("ident", [P, P])
        ones = sb("ones", [P, P])
        before = sb("before", [P, P])
        tile_base = sb("tile_base", [P, TT])
        node_id = sb("node_id", [P, TT])
        iota = sb("iota", [P, P])
        wa = [sb(f"wa{n}", [P, k, 2, 2 * HEADS], F32R) for n, k in ((1, KD), (2, KH))]
        wa_hi = [w[:, :, 0, :] for w in wa]
        wa_lo = [w[:, :, 1, :] for w in wa]
        att = [sb(f"att{n}", [P, TT, 2 * HEADS]) for n in (1, 2)]
        gates = att[0][:, 0:NT, :]
        self_count = sb("self_count", [P, TT])
        table = sb("table", [1, 3, TT], I32)

        gat_weights = ExitStack()

        def sbw(name, shape, dt=F32):
            return gat_weights.enter_context(nc.sbuf_tensor(name, shape, dt))

        w2_hi = sbw("w2_hi", [P, KH * H], F32R)
        w2_lo = sbw("w2_lo", [P, KH * H], F32R)
        fc_hi = sbw("fc_hi", [P, KH * D], F32R)
        fc_lo = sbw("fc_lo", [P, KH * D], F32R)

        early = ExitStack()

        def sbe(name, shape, dt=F32):
            return early.enter_context(nc.sbuf_tensor(name, shape, dt))

        w1_hi = sbe("w1_hi", [P, KD * H], F32R)
        w1_lo = sbe("w1_lo", [P, KD * H], F32R)
        stage = sbe("stage", [P, 2, H])
        att_vec = sbe("att_vec", [P, 2, H])
        prod = sbe("prod", [P, H])
        wa_f = [sbe(f"wa{n}_f", [P, k, 2 * HEADS]) for n, k in ((1, KD), (2, KH))]
        e_src = sbe("e_src", [P, EC], I32)
        e_dst = sbe("e_dst", [P, EC], I32)
        e_hi = sbe("e_hi", [P, EC])
        e_lo = sbe("e_lo", [P, EC])
        e_tmp = sbe("e_tmp", [P, EC], I32)
        e_other = sbe("e_other", [P, EC])
        e_self = sbe("e_self", [P, EC])
        e_count = sbe("e_count", [P, EC])
        e_pos = sbe("e_pos", [P, EC], I32)
        e_row = sbe("e_row", [P, EC, 2], I32)
        nowhere = sbe("nowhere", [P, 2 * EC], I32)
        zeros_e = sbe("zeros_e", [P, EC])
        before_me = sbe("before_me", [P, 1])
        pos_col = sbe("pos_col", [P, 4, 1], I32)
        row_col = sbe("row_col", [P, 4, 2], I32)
        hot_lo = sbe("hot_lo", [P, 4, P], BF16)
        hot_hi = sbe("hot_hi", [P, 4, 2 * TT], BF16)
        zero_b = sbe("zero_b", [P, 2 * TT], BF16)
        other_count = sbe("other_count", [P, TT])
        tile_sum = sbe("tile_sum", [P, TT])
        tile_scan = sbe("tile_scan", [P, TT])
        loops_f = sbe("loops_f", [1, TT])
        loops_i = sbe("loops_i", [1, TT], I32)
        loops_scan = sbe("loops_scan", [1, TT])
        x_in = sbe("x_in", [P, 2, D])
        x_norm = sbe("x_norm", [P, 2, D])
        ln_stats = sbe("ln_stats", [P, 2, 6])
        ln_mv = sbe("ln_mv", [P, 2, 2])
        ln_std = sbe("ln_std", [P, 2, 1])
        ln_rstd = sbe("ln_rstd", [P, 2, 1])
        ln_step = sbe("ln_step", [P, 2, 1])
        eps_col = sbe("eps_col", [P, 1])
        xT_hi = sbe("xT_hi", [P, 2, D], F32R)
        xT_lo = sbe("xT_lo", [P, 2, D], F32R)
        h_out = sbe("h_out", [P, 2, H])

        consts = sem("consts")
        cleared = sem("cleared")
        edges_in = sem("edges_in")
        w_in = [sem("w_in0"), sem("w_in1")]
        late_in = [sem("late_in0"), sem("late_in1")]
        w_hi_done = sem("w_hi_done")
        w_lo_done = sem("w_lo_done")
        att_in = [sem("att_in1"), sem("att_in2")]
        fill_done = sem("fill_done")
        parts_ready = sem("parts_ready")
        parts_summed = sem("parts_summed")
        rows_ready = sem("rows_ready")
        col_copied = sem("col_copied")
        scattered = [sem(f"scattered{n}") for n in range(4)]
        hot_ready = sem("hot_ready")
        hot_used = sem("hot_used")
        counts_done = sem("counts_done")
        table_done = sem("table_done")
        x_got = [sem("x_got0"), sem("x_got1")]
        std_ready = sem("std_ready")
        mv_ready = sem("mv_ready")
        xn_ready = sem("xn_ready")
        xt_ready = sem("xt_ready")
        xhi_ready = sem("xhi_ready")
        xlo_ready = sem("xlo_ready")
        h1_ready = sem("h1_ready")
        h1_left = sem("h1_left")
        h1_right = sem("h1_right")
        h1_stored = [sem("h1_stored0"), sem("h1_stored1")]
        att_stored = sem("att_stored")
        early.close()

        gat = ExitStack()

        def sbg(name, shape, dt=F32):
            return gat.enter_context(nc.sbuf_tensor(name, shape, dt))

        ix = sbg("ix", [P, 2, 2, 2], I32)
        dst_row = sbg("dst_row", [P, 2, C0 + C1, 2], I32)
        at_tile = sbg("at_tile", [P, 2, 2])
        off_tile = sbg("off_tile", [P, 2, 2])
        drop = sbg("drop", [P, 2, 2])
        src_ok = sbg("src_ok", [P, 2, 2, 1], I32)
        near_att = sbg("near_att", [P, 2, 2, 2 * HEADS])
        near_h = [sbg(f"near_h{c}", [P, 2, H]) for c in range(2)]
        diag = [sbg("diag0", [P, HEADS, C0]), sbg("diag1", [P, HEADS, C1])]
        hot_t = sbg("hot_t", [P, 2 * P])
        miss = sbg("miss", [P, C0 + C1])
        seen = sbg("seen", [P, HEADS, C0 + C1])
        hot = sbg("hot", [P, 2, P], F32R)
        hot1 = sbg("hot1", [P, 2, P], F32R)
        top = sbg("top", [P, HEADS])
        m_top = sbg("m_top", [P, HEADS])
        x_maxima = sbg("x_maxima", [P, 2 * HEADS])
        maxima = sbg("maxima", [P, 2 * HEADS])
        e_in = sbg("e_in", [P, 2, HEADS])
        e_own = sbg("e_own", [P, 2, HEADS])
        weight = sbg("weight", [P, 2, HEADS])
        weight_own = sbg("weight_own", [P, 2, HEADS])
        msg_hi = [sbg(f"msg{c}_hi", [P, H], F32R) for c in range(2)]
        msg_lo = [sbg("msg0_lo", [P, H], F32R)]
        with nc.sbuf_tensor("msg1_lo", [P, H], F32R) as msg1_lo:
            msg_lo.append(msg1_lo)
        msg_whole = sbg("msg_whole", [P, H])
        own = sbg("own", [P, 2, H])
        own_msg = sbg("own_msg", [P, H])
        denom = sbg("denom", [P, HEADS])
        gathered = sbg("gathered", [P, H])
        act_hi = sbg("act_hi", [P, H], F32R)
        act_lo = sbg("act_lo", [P, H], F32R)
        result = sbg("result", [P, 2, H])
        bias_row = sbg("bias_row", [P, H])
        m_ix = sbg("m_ix", [P, 2], I32)
        m_row = sbg("m_row", [P, P, 2], I32)
        m_small = sbg("m_small", [P, 2])
        m_src = sbg("m_src", [P, 1], I32)
        m_att = sbg("m_att", [P, 2 * HEADS])
        m_diag = sbg("m_diag", [P, HEADS, P])
        m_miss = sbg("m_miss", [P, P])
        x_ix = sbg("x_ix", [P, 2], I32)
        x_row = sbg("x_row", [P, P, 2], I32)
        x_small = sbg("x_small", [P, 3])
        x_src = sbg("x_src", [P, 1], I32)
        x_att = sbg("x_att", [P, 2 * HEADS])
        x_h = sbg("x_h", [P, H])
        x_hot_t = sbg("x_hot_t", [P, P])
        x_hot = sbg("x_hot", [P, P])
        x_e = sbg("x_e", [P, HEADS])
        x_weight = sbg("x_weight", [P, HEADS])
        x_msg = sbg("x_msg", [P, H])
        fcb_row = sbg("fcb_row", [P, D])
        x_plus = sbg("x_plus", [P, D])
        ln2 = sbg("ln2", [P, 16])
        ln_scale = sbg("ln_scale", [P, 2, 2])
        xT = sbg("xT", [P, D])
        gate_cols = sbg("gate_cols", [P, KD, EXPERTS])
        half_neg = sbg("half_neg", [P, 1])

        phase = sem("phase")
        small_in = sem("small_in")

        class Layer:

            def __init__(self, n):
                def s(name):
                    return sem(f"{name}_{n}")
                self.listed = [s("listed0"), s("listed1")]
                self.src_ready = s("src_ready")
                self.att_got = [s("att_got0"), s("att_got1")]
                self.h_got = [s("h_got0"), s("h_got1")]
                self.own_got = [s("own_got0"), s("own_got1")]
                self.diag_ready = s("diag_ready")
                self.spread = s("spread")
                self.max_ready = s("max_ready")
                self.at_edges = s("at_edges")
                self.e_ready = s("e_ready")
                self.weighed = s("weighed")
                self.msg_ready = s("msg_ready")
                self.own_ready = s("own_ready")
                self.summed = s("summed")
                self.denom_read = s("denom_read")
                self.gathered_ready = s("gathered_ready")
                self.turned = s("turned")
                self.hi_ready = s("hi_ready")
                self.lo_ready = s("lo_ready")
                self.first_done = s("first_done")
                self.second_done = s("second_done")
                self.copied = s("copied")
                self.extra_read = s("extra_read")
                self.stored = [s("stored0"), s("stored1")]
                self.m_listed = s("m_listed")
                self.m_src_ready = s("m_src_ready")
                self.m_got = s("m_got")
                self.m_diag_ready = s("m_diag_ready")
                self.m_spread = s("m_spread")
                self.m_used = s("m_used")
                self.x_listed = s("x_listed")
                self.x_src_ready = s("x_src_ready")
                self.x_got = s("x_got")
                self.x_at_edges = s("x_at_edges")
                self.x_e_ready = s("x_e_ready")
                self.x_msg_ready = s("x_msg_ready")
                self.x_used = s("x_used")

        layers = [Layer(1), Layer(2)]
        bias_in = sem("bias_in")
        x_again_got = sem("x_again_got")
        x_plus_ready = sem("x_plus_ready")
        var_ready = sem("var_ready")
        pow_ready = sem("pow_ready")
        scale_ready = sem("scale_ready")
        xn2_ready = sem("xn2_ready")
        xn2_turned = sem("xn2_turned")
        xT_ready = sem("xT_ready")
        gates_done = sem("gates_done")
        gat.close()
        gat_weights.close()

        route = ExitStack()

        def sbr(name, shape, dt=F32):
            return route.enter_context(nc.sbuf_tensor(name, shape, dt))

        NB = EXPERTS * BLOCKS
        ew_hi = sbr("ew_hi", [P, EXPERTS, KD, D], F32R)
        ew_lo = sbr("ew_lo", [P, EXPERTS, KD, D], F32R)
        ew_in = sbr("ew_in", [P, 2, KD, D])
        logp = sbr("logp", [P, NT, EXPERTS])
        work = sbr("work", [P, NT, EXPERTS])
        prob = sbr("prob", [P, NT, EXPERTS])
        above = sbr("above", [P, NT, EXPERTS])
        tie = sbr("tie", [P, NT, EXPERTS])
        above_b = sbr("above_b", [P, NT, EXPERTS], BF16)
        tie_b = sbr("tie_b", [P, NT, EXPERTS], BF16)
        scan = sbr("scan", [P, NT, EXPERTS])
        place = sbr("place", [P, NT, EXPERTS])
        place_i = sbr("place_i", [P, NT, EXPERTS], I32)
        place_hi = sbr("place_hi", [P, NT, EXPERTS])
        place_lo = sbr("place_lo", [P, NT, EXPERTS], BF16)
        iota_b = sbr("iota_b", [P, P], BF16)
        code = sbr("code", [P, NT, EXPERTS])
        row_a = sbr("row_a", [P, NT])
        row_b = sbr("row_b", [P, NT])
        outside = sbr("outside", [P, NT])
        inside = sbr("inside", [P, 1])
        outside_neg = sbr("outside_neg", [P, 1])
        tile_no = sbr("tile_no", [P, NT])
        ones_b = sbr("ones_b", [P, P], BF16)
        before_b = sbr("before_b", [P, P], BF16)
        col_a = sbr("col_a", [P, EXPERTS])
        col_b = sbr("col_b", [P, EXPERTS])
        col_c = sbr("col_c", [P, EXPERTS])
        col_t = sbr("col_t", [EXPERTS, 1])
        col_diag = sbr("col_diag", [EXPERTS, EXPERTS])
        bit = sbr("bit", [P, EXPERTS], I32)
        found = sbr("found", [P, EXPERTS], I32)
        trial = sbr("trial", [P, EXPERTS], I32)
        zeros_r = sbr("zeros_r", [P, NT])
        zero_rb = sbr("zero_rb", [P, EXPERTS * 3 * BLOCKS], BF16)
        place_hot = sbr("place_hot", [P, 2, EXPERTS, P], BF16)
        block_hot = sbr("block_hot", [P, 2, EXPERTS, BLOCKS])
        block_val = sbr("block_val", [P, 2, EXPERTS, 3, BLOCKS], BF16)
        listed_f = sbr("listed_f", [P, EXPERTS, 3, BLOCKS])
        token_f = sbr("token_f", [P, EXPERTS, BLOCKS])
        token = sbr("token", [P, NB, 1], I32)
        factor = sbr("factor", [P, NB, 1])
        past_end = sbr("past_end", [P, 1])
        fetch_at = sbr("fetch_at", [P, 2, 1], I32)
        add_at = sbr("add_at", [P, 2, 1], I32)
        x_tok = ew_in[:, 0, 0:2, :]
        y_tok = ew_in[:, 0, 2:4, :]
        tT_hi = sbr("tT_hi", [P, 2, D], F32R)
        tT_lo = sbr("tT_lo", [P, 2, D], F32R)

        ew_got = [sem("ew_got0"), sem("ew_got1")]
        ew_hi_done = sem("ew_hi_done")
        ew_lo_done = sem("ew_lo_done")
        to_log = sem("to_log")
        from_log = sem("from_log")
        share_ready = sem("share_ready")
        share_done = sem("share_done")
        hots_ready = sem("hots_ready")
        vals_ready = sem("vals_ready")
        hots_used = sem("hots_used")
        lists_ready = sem("lists_ready")
        fetch_ready = sem("fetch_ready")
        tok_got = [sem("tok_got0"), sem("tok_got1")]
        tok_turned = sem("tok_turned")
        tok_hi = sem("tok_hi")
        tok_lo = sem("tok_lo")
        tok_done = sem("tok_done")
        add_ready = sem("add_ready")
        y_ready = sem("y_ready")
        added = sem("added")
        route.close()

        passed = sem("passed")

        block = ctx.enter_context(nc.Block())

        def piece_of(w, k):
            if w.shape[1] == D:
                return w.rearrange("(k p) n -> p k n", p=P)[:, 2 * k:2 * k + 2, :]
            return w.rearrange("(k p) n -> p k n", p=P)[:, k:k + 1, :]

        def staged(n, w):
            return stage[:, n % 2, :].rearrange("p (k n) -> p k n", n=w.shape[1])

        def more_chunks(eng, t, body):
            count = eng.value_load(table[0:1, 1, bass.ds(t.n, 1)], min_val=0, max_val=E // P + 1)
            with eng.If(count > 0):
                before_it = eng.value_load(table[0:1, 2, bass.ds(t.n, 1)], min_val=0, max_val=E // P + 1)
                with eng.Fori(0, count) as j:
                    body(before_it + j, j)

        @block.sync
        def _(sp):
            sp.wait_ge(cleared, 2)
            for e, given in ((e_src, src), (e_dst, dst)):
                sp.dma_start(e[0:EROWS, :], given[0:EROWS * EC].rearrange("(p j) -> p j", j=EC)).then_inc(edges_in, 16)
                sp.dma_start(e[EROWS:EROWS + 1, 0:EREST], given[EROWS * EC:E].rearrange("(o j) -> o j", o=1)).then_inc(edges_in, 16)
            for n in range(KD):
                if n >= 2:
                    sp.wait_ge(w_hi_done, n - 1)
                    sp.wait_ge(w_lo_done, n - 1)
                sp.dma_start(staged(n, W1), piece_of(W1, n)).then_inc(w_in[n % 2], 16)
                if n == 0:
                    for m, a in enumerate((att_src1, att_dst1)):
                        sp.dma_start(att_vec[:, m, :], a.rearrange("(o h) c -> o (h c)", o=1).to_broadcast((P, H))).then_inc(att_in[0], 16)
            sp.wait_ge(w_lo_done, KD)
            for m, a in enumerate((att_src2, att_dst2)):
                sp.dma_start(att_vec[:, m, :], a.rearrange("(o h) c -> o (h c)", o=1).to_broadcast((P, H))).then_inc(att_in[1], 16)

            def store_h1(t):
                if t is None:
                    return
                sp.wait_ge(h1_left, t.n + 1)
                sp.wait_ge(h1_right, t.n + 1)
                sp.dma_start(h_rows[0][bass.ds(t.n * P, P), :], h_out[:, t.s, :]).then_inc(h1_stored[t.s], 16)

            def load_x(t):
                if t is None:
                    return
                if not t.early(2):
                    sp.wait_ge(xn_ready, t.n - 1)
                rows = P if not (isinstance(t.n, int) and t.n == NT - 1) else LAST
                sp.dma_start(x_in[0:rows, t.s, :], x[bass.ds(t.n * P, rows), :]).then_inc(x_got[t.s], 16)

            def step(s):
                store_h1(s(-1))
                load_x(s(3))
            steps(sp, step, 3, 1)
            sp.dma_start(att_rows[0].rearrange("(t p) a -> p t a", p=P), att[0][:, 0:NT, :]).then_inc(att_stored, 16)
            for n in range(2):
                sp.wait_ge(h1_stored[n], 16 * ((NT + 1 - n) // 2))
            sp.wait_ge(att_stored, 16)
            sp.sem_inc(phase, 1)
            sp.wait_ge(phase, 5)

            sp.dma_start(fcb_row[:], fcb.rearrange("(o n) -> o n", o=1).to_broadcast((P, D))).then_inc(small_in, 16)
            sp.dma_start(gate_cols[:], gate_w[0].rearrange("(k p) e -> p k e", p=P)).then_inc(small_in, 16)

            def gat_layer(n, L):
                sp.dma_start(bias_row[:], (b1, b2)[n].rearrange("(o n) -> o n", o=1).to_broadcast((P, H))).then_inc(bias_in, 16)

                def lists(t):
                    if t is None:
                        return
                    first = sp.value_load(table[0:1, 0, bass.ds(t.n, 1)], min_val=0, max_val=E)
                    if not t.early(2):
                        sp.wait_ge(L.max_ready, t.n - 1)
                    rows = packed[bass.ds(first, 2 * P), :]
                    sp.dma_start(ix[:, t.s, :, :], rows.rearrange("(c p) w -> p c w", p=P)).then_inc(L.listed[t.s], 16)
                    sp.dma_start(dst_row[:, t.s, :, :].rearrange("p e w -> p (e w)"),
                                 packed[bass.ds(first, C0 + C1), :].rearrange("(o e) w -> o (e w)", o=1).to_broadcast((P, 2 * (C0 + C1)))).then_inc(L.listed[t.s], 16)

                def own_rows(t):
                    if t is None:
                        return
                    if not t.early(2):
                        sp.wait_ge(L.gathered_ready, t.n - 1)
                    sp.dma_start(own[:, t.s, :], h_rows[n][bass.ds(t.n * P, P), :]).then_inc(L.own_got[t.s], 16)

                def x_rows(t):
                    if t is None or n == 0:
                        return
                    if not t.early(1):
                        sp.wait_ge(L.copied, t.n)
                    else:
                        sp.wait_ge(consts, 2)
                    rows = P if not (isinstance(t.n, int) and t.n == NT - 1) else LAST
                    sp.dma_start(x_plus[0:rows, :], x[bass.ds(t.n * P, rows), :]).then_inc(x_again_got, 16)

                def more_lists(t, to, listed, used):
                    if t is None:
                        return

                    def body(v, j):
                        first = sp.value_load(table[0:1, 0, bass.ds(t.n, 1)], min_val=0, max_val=E)
                        start = nc.s_assert_within(first + j * P + (C0 + C1), 0, E + P, skip_runtime_bounds_check_because="a tile's chunks end at most a chunk past the last edge")
                        rows = packed[bass.ds(start, P), :]
                        sp.wait_ge(used, v + 1)
                        sp.dma_start(to[0][:], rows).then_inc(listed, 16)
                        sp.dma_start(to[1][:].rearrange("p e w -> p (e w)"),
                                     rows.rearrange("(o e) w -> o (e w)", o=1).to_broadcast((P, 2 * P))).then_inc(listed, 16)
                    more_chunks(sp, t, body)

                def store(t):
                    if t is None:
                        return
                    if n == 0:
                        sp.wait_ge(L.copied, 2 * (t.n + 1))
                        sp.dma_start(h_rows[1][bass.ds(t.n * P, P), :], result[:, t.s, :]).then_inc(L.stored[t.s], 16)
                    else:
                        sp.wait_ge(xn2_ready, t.n + 1)
                        rows = P if not (isinstance(t.n, int) and t.n == NT - 1) else LAST
                        sp.dma_start(out[bass.ds(t.n * P, rows), :], result[0:rows, t.s, 0:D]).then_inc(L.stored[t.s], 16)
                        sp.dma_start(xn_rows[bass.ds(t.n * P, rows), :], result[0:rows, t.s, D:2 * D]).then_inc(L.stored[t.s], 16)

                def step(s):
                    more_lists(s(2), (m_ix, m_row), L.m_listed, L.m_used)
                    more_lists(s(1), (x_ix, x_row), L.x_listed, L.x_used)
                    x_rows(s(0))
                    own_rows(s(2))
                    store(s(-1))
                    lists(s(4))
                steps(sp, step, 4, 1)
                for m in range(2):
                    sp.wait_ge(L.stored[m], 16 * (n + 1) * ((NT + 1 - m) // 2))
                if n == 0:
                    sp.wait_ge(L.extra_read, NT)
                    sp.dma_start(att_rows[1].rearrange("(t p) a -> p t a", p=P), att[1][:, 0:NT, :]).then_inc(att_stored, 16)
                    sp.wait_ge(att_stored, 32)
                sp.sem_inc(phase, 1)
                sp.wait_ge(phase, 10 + 5 * n)
            gat_layer(0, layers[0])
            gat_layer(1, layers[1])
            for e in range(EXPERTS):
                if e >= 2:
                    sp.wait_ge(ew_hi_done, e - 1)
                    sp.wait_ge(ew_lo_done, e - 1)
                sp.dma_start(ew_in[:, e % 2, :, :], experts[e].rearrange("(k p) n -> p k n", p=P)).then_inc(ew_got[e % 2], 16)
            sp.wait_ge(added, 16 * NB)

        @block.gpsimd
        def _(pool):
            pool.memset(e_src[:], NOWHERE).then_inc(cleared, 1)
            pool.memset(e_dst[:], NOWHERE).then_inc(cleared, 1)
            pool.memset(ident[:], 0.0)
            pool.memset(ones[:], 1.0)
            pool.memset(before[:], 1.0)
            pool.memset(zero_b[:], 0.0)
            pool.memset(zeros_e[:], 0.0)
            pool.memset(eps_col[:], EPS_LN)
            pool.iota(iota[:], pattern=[[1, P]], base=0, channel_multiplier=0, allow_small_or_imprecise_dtypes=True)
            pool.iota(tile_base[:], pattern=[[P, TT]], base=0, channel_multiplier=0, allow_small_or_imprecise_dtypes=True)
            pool.iota(node_id[:], pattern=[[P, TT]], base=0, channel_multiplier=1, allow_small_or_imprecise_dtypes=True)
            pool.drain()
            pool.affine_select(out=ident[:], in_=ident[:], compare_op=ALU.not_equal, fill=1.0, base=0,
                               pattern=[[-1, P]], channel_multiplier=1)
            pool.affine_select(out=before[:], in_=before[:], compare_op=ALU.is_gt, fill=0.0, base=0,
                               pattern=[[1, P]], channel_multiplier=-1)
            pool.drain().then_inc(consts, 1)

            pool.memset(nowhere[:], NOWHERE)
            pool.drain()
            pool.dma_start(packed[0:P * EC, :].rearrange("(p j) w -> p (j w)", p=P), nowhere[:]).then_inc(fill_done, 16)
            pool.dma_start(packed[P * EC:PACKED, :].rearrange("(p j) w -> p (j w)", p=P), nowhere[:, 0:8]).then_inc(fill_done, 16)
            pool.wait_ge(fill_done, 32)
            pool.wait_ge(rows_ready, 1)

            packed_end = pool.to_reg(PACKED - 1)

            def scatter(k, c, wait):
                slot = c % 4
                if wait is not None:
                    pool.wait_ge(scattered[slot], wait)
                    pool.sem_inc(passed, 1)
                pool.tensor_copy(pos_col[:, slot, :], e_pos[:, bass.ds(2 * k + c, 1)]).then_inc(col_copied, 1)
                pool.tensor_copy(row_col[:, slot, :], e_row[:, bass.ds(2 * k + c, 1), :].rearrange("p o w -> p (o w)")).then_inc(col_copied, 1)
                pool.wait_ge(col_copied, 2 * (2 * k + c) + 2)
                pool.sem_inc(passed, 1)
                pool.indirect_dma_start(out=packed, out_offset=bass.IndirectOffsetOnAxis(ap=pos_col[:, slot, :], axis=0),
                                        in_=row_col[:, slot, :], in_offset=None, bounds_check=packed_end, oob_is_err=False).then_inc(scattered[slot], 16)
            for c in range(4):
                scatter(0, c, None)
            with pool.Fori(1, EC // 4) as q:
                for c in range(4):
                    scatter(2 * q, c, 16 * q)
            for c in range(EC - EC // 4 * 4):
                scatter(2 * (EC // 4), c, 16 * (EC // 4))

            for m in range(4):
                pool.wait_ge(scattered[m], 16 * ((EC + 3 - m) // 4))

            pool.wait_ge(w_lo_done, KD)
            pool.wait_ge(att_in[1], 32)
            pieces = [(W2, w2_hi, w2_lo, k) for k in range(KH)] + [(fcW, fc_hi, fc_lo, k) for k in range(KH // 2)]
            for n, (w, hi, lo, k) in enumerate(pieces):
                cols = slice(k * H, (k + 1) * H)
                pool.dma_start(staged(n, w), piece_of(w, k)).then_inc(late_in[n % 2], 16)
                pool.wait_ge(late_in[n % 2], 16 * (n // 2 + 1))
                pool.tensor_copy(hi[:, cols], stage[:, n % 2, :])
                for m in range(2 if w is W2 else 0):
                    pool.tensor_tensor(prod[:], stage[:, n % 2, :], att_vec[:, m, :], ALU.mult)
                    by_head = prod[:].rearrange("p (h c) -> p h c", h=HEADS)
                    width = HID // 2
                    while width > 1:
                        pool.drain()
                        pool.tensor_tensor(by_head[:, :, 0:width], by_head[:, :, 0:width], by_head[:, :, width:2 * width], ALU.add)
                        width //= 2
                    pool.drain()
                    pool.tensor_tensor(wa_f[1][:, k, m * HEADS:(m + 1) * HEADS], by_head[:, :, 0], by_head[:, :, 1], ALU.add)
                    pool.drain()
                pool.drain()
                pool.tensor_tensor(lo[:, cols], stage[:, n % 2, :], hi[:, cols].bitcast(F32), ALU.subtract)
            pool.tensor_copy(wa_hi[1], wa_f[1][:])
            pool.drain()
            pool.tensor_tensor(wa_lo[1], wa_f[1][:], wa_hi[1].bitcast(F32), ALU.subtract)
            pool.drain().then_inc(phase, 1)
            pool.wait_ge(phase, 5)
            for m in range(2):
                pool.memset(near_h[m][:], 0.0)
            pool.memset(near_att[:], 0.0)
            pool.memset(hot_t[:], 0.0)
            pool.memset(m_att[:], 0.0)
            pool.memset(x_att[:], 0.0)
            pool.memset(x_h[:], 0.0)
            pool.memset(half_neg[:], -0.5)
            pool.memset(x_plus[:], 0.0)
            pool.drain().then_inc(consts, 1)
            nodes_end = pool.to_reg(NPAD - 1)

            def gat_layer(n, L):
                def fetch(to, rows_of, index, got):
                    pool.indirect_dma_start(out=to, out_offset=None, in_=rows_of,
                                            in_offset=bass.IndirectOffsetOnAxis(ap=index, axis=0),
                                            bounds_check=nodes_end, oob_is_err=False).then_inc(got, 16)

                def spread_diag(to, terms, rows):
                    one = ident[0:rows, 0:to.shape[2]].rearrange("p (o e) -> p o e", o=1).to_broadcast((rows, HEADS, to.shape[2]))
                    return pool.tensor_tensor(to[0:rows, :, :], one, terms.rearrange("p (h o) -> p h o", o=1).to_broadcast((rows, HEADS, to.shape[2])), ALU.mult)

                def gathers(t):
                    if t is None:
                        return
                    if not t.early(2):
                        pool.wait_ge(L.msg_ready, t.n - 1)
                        pool.wait_ge(L.weighed, 2 * (t.n - 1))
                        pool.sem_inc(passed, 1)
                    pool.wait_ge(L.src_ready, t.n + 1)
                    pool.sem_inc(passed, 1)
                    fetch(near_att[:, t.s, 0, :], att_rows[n], src_ok[:, t.s, 0, :], L.att_got[t.s])
                    fetch(near_att[0:C1, t.s, 1, :], att_rows[n], src_ok[0:C1, t.s, 1, :], L.att_got[t.s])
                    fetch(near_h[0][:, t.s, :], h_rows[n], src_ok[:, t.s, 0, :], L.h_got[t.s])
                    fetch(near_h[1][0:C1, t.s, :], h_rows[n], src_ok[0:C1, t.s, 1, :], L.h_got[t.s])

                def diagonals(t):
                    if t is None:
                        return
                    pool.wait_ge(L.att_got[t.s], 32 * (t.h + 1))
                    if not t.early(1):
                        pool.wait_ge(L.spread, t.n)
                    pool.sem_inc(passed, 1)
                    spread_diag(diag[0], near_att[:, t.s, 0, 0:HEADS], C0)
                    spread_diag(diag[1], near_att[0:C1, t.s, 1, 0:HEADS], C1)
                    pool.sem_inc(passed, 1)
                    pool.engine_nop().then_inc(L.diag_ready, 1)

                def own_messages(t):
                    if t is None:
                        return
                    pool.wait_ge(L.own_got[t.s], 16 * (t.h + 1))
                    pool.wait_ge(L.weighed, 2 * t.n + 1)
                    if not t.early(1):
                        pool.wait_ge(L.gathered_ready, t.n)
                    pool.sem_inc(passed, 1)
                    pool.tensor_tensor(own_msg[:].rearrange("p (h c) -> p h c", h=HEADS), own[:, t.s, :].rearrange("p (h c) -> p h c", h=HEADS),
                                       weight_own[:, t.s, :].rearrange("p (h o) -> p h o", o=1).to_broadcast((P, HEADS, HID)), ALU.mult).then_inc(L.own_ready, 1)

                def low(t):
                    if t is None or n == 0:
                        return
                    pool.wait_ge(L.hi_ready, 2 * t.n + 2)
                    pool.sem_inc(passed, 1)
                    pool.tensor_tensor(act_lo[:], gathered[:], act_hi[:].bitcast(F32), ALU.subtract).then_inc(L.lo_ready, 1)

                def m_body(v, j):
                    pool.wait_ge(L.m_src_ready, v + 1)
                    pool.sem_inc(passed, 1)
                    fetch(m_att[:], att_rows[n], m_src[:], L.m_got)
                    pool.wait_ge(L.m_got, 16 * (v + 1))
                    pool.sem_inc(passed, 1)
                    spread_diag(m_diag, m_att[:, 0:HEADS], P).then_inc(L.m_diag_ready, 1)

                def x_body(v, j):
                    pool.wait_ge(L.x_src_ready, v + 1)
                    pool.sem_inc(passed, 1)
                    fetch(x_att[:], att_rows[n], x_src[:], L.x_got)
                    fetch(x_h[:], h_rows[n], x_src[:], L.x_got)

                def plus(t):
                    if t is None or n == 0:
                        return
                    pool.wait_ge(x_again_got, 16 * (t.n + 1))
                    if t.early(1):
                        pool.wait_ge(small_in, 32)
                    pool.sem_inc(passed, 1)
                    pool.tensor_tensor(x_plus[:], x_plus[:], fcb_row[:], ALU.add).then_inc(x_plus_ready, 1)

                def power(t):
                    if t is None or n == 0:
                        return
                    pool.wait_ge(var_ready, t.n + 1)
                    pool.sem_inc(passed, 1)
                    pool.tensor_tensor(ln2[:, 9:10], ln2[:, 8:9], half_neg[:], ALU.pow).then_inc(pow_ready, 1)

                def step(s):
                    own_messages(s(1))
                    if n == 0:
                        gathers(s(3))
                    low(s(0))
                    power(s(-1))
                    if s(2) is not None:
                        more_chunks(pool, s(2), m_body)
                    if s(1) is not None:
                        more_chunks(pool, s(1), x_body)
                    if n == 1:
                        gathers(s(3))
                    plus(s(0))
                    diagonals(s(3))
                steps(pool, step, 3, 1)
                pool.drain().then_inc(phase, 1)
                pool.wait_ge(phase, 10 + 5 * n)
            gat_layer(0, layers[0])
            gat_layer(1, layers[1])
            pool.memset(ones_b[:], 1.0)
            pool.memset(zeros_r[:], 0.0)
            pool.memset(zero_rb[:], 0.0)
            pool.memset(bit[:], 1 << (FLOAT_BITS - 1))
            pool.memset(found[:], 0)
            pool.tensor_copy(before_b[:], before[:])
            pool.tensor_copy(iota_b[:], iota[:])
            pool.tensor_scalar(outside[:], node_id[:, 0:NT], float(N), None, ALU.is_ge)
            pool.tensor_scalar(inside[:], node_id[:, NT - 1:NT], float(N), None, ALU.is_lt)
            pool.tensor_scalar(outside_neg[:], node_id[:, NT - 1:NT], float(N), -BIG, ALU.is_ge, ALU.mult)
            pool.tensor_scalar(past_end[:], node_id[:, 0:1], float(LAST_ROWS), None, ALU.is_ge)
            pool.tensor_scalar(tile_no[:], tile_base[:, 0:NT], 1.0 / P, None, ALU.mult)
            pool.drain().then_inc(consts, 1)
            for e in range(EXPERTS):
                pool.wait_ge(ew_hi_done, e + 1)
                pool.tensor_tensor(ew_lo[:, e, :, :], ew_in[:, e % 2, :, :], ew_hi[:, e, :, :].bitcast(F32), ALU.subtract).then_inc(ew_lo_done, 1)

            def block_values(t):
                if t is None:
                    return
                pool.wait_ge(hots_ready, t.n + 1)
                pool.sem_inc(passed, 1)
                one = block_hot[:, t.s, :, :]
                code_of = code[:, bass.ds(t.n, 1), :].rearrange("p o e -> p (e o)")
                values = (tile_no[:, bass.ds(t.n, 1)], node_id[:, 0:1], code_of)
                for v, value in enumerate(values):
                    value = value.rearrange("p (e o) -> p e o", o=1).to_broadcast((P, EXPERTS, BLOCKS))
                    mm = pool.tensor_tensor(block_val[:, t.s, :, v, :], one, value, ALU.mult)
                mm.then_inc(vals_ready, 1)

            def step(s):
                block_values(s(0))
            steps(pool, step, 0)
            tokens_end = pool.to_reg(N - 1)
            pool.wait_ge(ew_lo_done, EXPERTS)

            def fetch(t):
                if t is None:
                    return
                if not t.early(2):
                    pool.wait_ge(tok_turned, t.n - 1)
                    pool.sem_inc(passed, 1)
                pool.wait_ge(fetch_ready, t.n + 1)
                pool.sem_inc(passed, 1)
                pool.indirect_dma_start(out=x_tok[:, t.s, :], out_offset=None, in_=xn_rows,
                                        in_offset=bass.IndirectOffsetOnAxis(ap=fetch_at[:, t.s, :], axis=0),
                                        bounds_check=tokens_end, oob_is_err=False).then_inc(tok_got[t.s], 16)

            def add(t):
                if t is None:
                    return
                pool.wait_ge(y_ready, t.n + 1)
                pool.wait_ge(add_ready, t.n + 1)
                if not t.early(1):
                    pool.wait_ge(added, 16 * t.n)
                pool.sem_inc(passed, 1)
                pool.indirect_dma_start(out=out, out_offset=bass.IndirectOffsetOnAxis(ap=add_at[:, t.s, :], axis=0),
                                        in_=y_tok[:, t.s, :], in_offset=None, bounds_check=tokens_end, oob_is_err=True,
                                        compute_op=ALU.add).then_inc(added, 16)

            def step(s):
                fetch(s(2))
                add(s(-1))
            steps(pool, step, 2, 1, NB)

        @block.scalar
        def _(act):
            for n in range(KD):
                act.wait_ge(w_in[n % 2], 16 * (n // 2 + 1))
                act.activation(w1_hi[:, n * H:(n + 1) * H], stage[:, n % 2, :], ACT.Copy).then_inc(w_hi_done, 1)
            act.wait_ge(consts, 1)

            def deviation(t):
                if t is None:
                    return
                act.wait_ge(mv_ready, t.n + 1)
                act.activation(ln_std[:, t.s, :], ln_mv[:, t.s, 1:2], ACT.Sqrt, bias=eps_col[:, 0:1]).then_inc(std_ready, 1)

            def high(t):
                if t is None:
                    return
                act.wait_ge(xt_ready, t.n + 1)
                if not t.early(2):
                    act.wait_ge(h1_ready, t.n - 1)
                act.activation(xT_hi[:, t.s, :], ps[1][:, t.s * 512:t.s * 512 + 512], ACT.Copy).then_inc(xhi_ready, 1)

            def left(t):
                if t is None:
                    return
                act.wait_ge(h1_ready, t.n + 1)
                if not t.early(2):
                    act.wait_ge(h1_stored[t.s], 16 * t.h)
                act.activation(h_out[:, t.s, 0:512], ps[2 * t.s][:, 0:512], ACT.Copy).then_inc(h1_left, 1)

            def step(s):
                left(s(-1))
                deviation(s(2))
                high(s(1))
            steps(act, step, 2, 1)
            act.drain().then_inc(phase, 1)
            act.wait_ge(phase, 5)

            def gat_layer(n, L):
                def by_head(to, rows, h, w):
                    for m in range(HEADS):
                        act.activation(to[0:rows, m * HID:(m + 1) * HID], h[0:rows, m * HID:(m + 1) * HID], ACT.Copy, scale=w[0:rows, m:m + 1])

                def high(t):
                    if t is None:
                        return
                    act.wait_ge(L.turned, t.n + 1)
                    if not t.early(1):
                        act.wait_ge(L.second_done, t.n)
                    act.activation(act_hi[:], ps[1][:], ACT.Relu).then_inc(L.hi_ready, 1)
                    if n == 1:
                        act.activation(gathered[:], ps[1][:], ACT.Relu).then_inc(L.hi_ready, 1)

                def x_body(v, j):
                    act.wait_ge(L.x_e_ready, v + 1)
                    act.activation(x_weight[:], x_e[:], ACT.Exp, bias=x_small[:, 2:3])
                    act.drain()
                    by_head(x_msg, P, x_h, x_weight)
                    act.drain().then_inc(L.x_msg_ready, 1)

                def copy_out(t, half):
                    if t is None or n == 1:
                        return
                    act.wait_ge((L.first_done, L.second_done)[half], t.n + 1)
                    if half == 0 and not t.early(2):
                        act.wait_ge(L.stored[t.s], 16 * t.h)
                    act.activation(result[:, t.s, half * 512:half * 512 + 512], ps[0][:, half * 512:half * 512 + 512], ACT.Copy).then_inc(L.copied, 1)

                def normalised(r):
                    if r is None or n == 0:
                        return
                    act.wait_ge(scale_ready, r.n + 1)
                    act.activation(result[:, r.s, D:2 * D], result[:, r.s, 0:D], ACT.Identity, bias=ln_scale[:, r.s, 1:2], scale=ln_scale[:, r.s, 0:1]).then_inc(xn2_ready, 1)

                def messages(t, r):
                    if t is None:
                        normalised(r)
                        return
                    act.wait_ge(L.e_ready, t.n + 1)
                    act.wait_ge(L.h_got[t.s], 32 * (t.h + 1))
                    if not t.early(1):
                        act.wait_ge(L.summed, t.n)
                    act.activation(weight_own[:, t.s, :], e_own[:, t.s, :], ACT.Exp)
                    for c in range(2):
                        act.activation(weight[:, c, :], e_in[:, c, :], ACT.Exp, bias=drop[:, t.s, c:c + 1])
                    act.drain()
                    act.activation(weight_own[:, t.s, :], weight_own[:, t.s, :], ACT.Copy, scale=self_count[:, bass.ds(t.n, 1)])
                    by_head(msg_hi[0], C0, near_h[0][:, t.s, :], weight[:, 0, :])
                    act.drain().then_inc(L.weighed, 1)
                    normalised(r)
                    by_head(msg_hi[1] if n == 0 else msg_whole, C1, near_h[1][:, t.s, :], weight[:, 1, :])
                    act.drain().then_inc(L.weighed, 1)

                def gate_input(t):
                    if t is None or n == 0:
                        return
                    act.wait_ge(xn2_turned, t.n + 1)
                    if not t.early(1):
                        act.wait_ge(gates_done, t.n)
                    act.activation(xT[:], ps[0][:, 512:1024], ACT.Copy).then_inc(xT_ready, 1)

                def step(s):
                    copy_out(s(-1), 1)
                    gate_input(s(-2))
                    high(s(0))
                    copy_out(s(0), 0)
                    if s(1) is not None:
                        more_chunks(act, s(1), x_body)
                    messages(s(2), s(-1))
                steps(act, step, 2, 2)
                act.drain().then_inc(phase, 1)
                act.wait_ge(phase, 10 + 5 * n)
            gat_layer(0, layers[0])
            gat_layer(1, layers[1])
            act.wait_ge(consts, 3)
            act.wait_ge(to_log, 1)
            act.activation(logp[:], work[:], ACT.Ln).then_inc(from_log, 1)

            def split(e):
                act.wait_ge(ew_got[e % 2], 16 * (e // 2 + 1))
                act.activation(ew_hi[:, e, :, :], ew_in[:, e % 2, :, :], ACT.Copy).then_inc(ew_hi_done, 1)

            for i in range(SINKHORN_ITERS):
                act.wait_ge(to_log, 3 * i + 2)
                act.activation(work[:], work[:], ACT.Exp).then_inc(from_log, 1)
                act.wait_ge(share_done, 3 * i + 3)
                act.activation(col_b[:], ps[3][:, 520:528], ACT.Ln).then_inc(from_log, 1)
                if i < EXPERTS:
                    split(i)
                act.wait_ge(to_log, 3 * i + 3)
                act.activation(work[:], work[:], ACT.Exp).then_inc(from_log, 1)
                act.wait_ge(to_log, 3 * i + 4)
                act.activation(row_b[:], row_b[:], ACT.Ln).then_inc(from_log, 1)
            for e in range(SINKHORN_ITERS, EXPERTS):
                split(e)
            act.wait_ge(to_log, 3 * SINKHORN_ITERS + 2)
            act.activation(prob[:], logp[:], ACT.Exp).then_inc(from_log, 1)

            def high(t):
                if t is None:
                    return
                act.wait_ge(tok_turned, t.n + 1)
                if not t.early(2):
                    act.wait_ge(tok_done, t.n - 1)
                act.activation(tT_hi[:, t.s, :], ps[1][:, t.s * 512:t.s * 512 + 512], ACT.Copy).then_inc(tok_hi, 1)

            def scale(t):
                if t is None:
                    return
                act.wait_ge(tok_done, t.n + 1)
                if t.early(1):
                    act.wait_ge(lists_ready, 1)
                    act.wait_ge(ew_lo_done, EXPERTS)
                if not t.early(2):
                    act.wait_ge(added, 16 * (t.n - 1))
                act.activation(y_tok[:, t.s, :], ps[2 * t.s][:, 0:512], ACT.Copy, scale=factor[:, bass.ds(t.n, 1), :].rearrange("p o w -> p (o w)")).then_inc(y_ready, 1)

            def step(s):
                scale(s(-1))
                high(s(1))
            steps(act, step, 1, 1, NB)

        @block.tensor
        def _(pe):
            pe.wait_ge(consts, 1)
            pe.wait_ge(parts_ready, 1)
            pe.matmul(ps[3][:, 512:513], before[:], before_me[:], start=True, stop=True).then_inc(parts_summed, 1)
            pe.matmul(ps[3][:, 0:2 * TT], zero_b[:, 0:P], zero_b[:], start=True, stop=False)

            def transposes(t):
                if t is None:
                    return
                pe.wait_ge(xn_ready, t.n + 1)
                if not t.early(2):
                    pe.wait_ge(xlo_ready, t.n - 1)
                for k in range(KD):
                    mm = pe.transpose(ps[1][:, t.s * 512 + k * P:t.s * 512 + (k + 1) * P], x_norm[:, t.s, k * P:(k + 1) * P], ident[:])
                mm.then_inc(xt_ready, 1)

            def counts(t):
                if t is None:
                    return
                pe.wait_ge(hot_ready, t.n + 1)
                for u in range(2):
                    mm = pe.matmul(ps[3][:, 0:2 * TT], hot_lo[:, 2 * t.s + u, :], hot_hi[:, 2 * t.s + u, :], start=False, stop=False)
                mm.then_inc(hot_used, 1)

            def products(t):
                if t is None:
                    return
                pe.wait_ge(xlo_ready, t.n + 1)
                if not t.early(2):
                    pe.wait_ge(h1_left, t.n - 1)
                    pe.wait_ge(h1_right, t.n - 1)
                if t.early(1):
                    pe.wait_ge(w_lo_done, KD)
                    pe.wait_ge(w_hi_done, KD)
                o = ps[2 * t.s]
                for half in range(2):
                    for k in range(KD):
                        w = slice(k * H + half * 512, k * H + half * 512 + 512)
                        a = slice(k * P, (k + 1) * P)
                        cols = o[:, half * 512:half * 512 + 512]
                        pe.matmul(cols, xT_hi[:, t.s, a], w1_hi[:, w], start=(k == 0), stop=False)
                        pe.matmul(cols, xT_hi[:, t.s, a], w1_lo[:, w], start=False, stop=False)
                        pe.matmul(cols, xT_lo[:, t.s, a], w1_hi[:, w], start=False, stop=(k == KD - 1))
                cols = ps[3][:, 512:528]
                if not t.early(1):
                    pe.wait_ge(h1_right, t.n)
                for k in range(KD):
                    a = slice(k * P, (k + 1) * P)
                    pe.matmul(cols, xT_hi[:, t.s, a], wa[0][:, k, :, :].rearrange("p v a -> p (v a)"), start=(k == 0), stop=False)
                    mm = pe.matmul(cols[:, 0:8], xT_lo[:, t.s, a], wa_hi[0][:, k, :], start=False, stop=(k == KD - 1))
                mm.then_inc(h1_ready, 1)

            def step(s):
                transposes(s(1))
                counts(s(0))
                products(s(0))
            steps(pe, step, 1)
            pe.matmul(ps[3][:, 0:2 * TT], zero_b[:, 0:P], zero_b[:], start=False, stop=True).then_inc(counts_done, 1)
            pe.wait_ge(parts_ready, 2)
            pe.matmul(ps[3][:, 512:512 + TT], ones[:], other_count[:], start=True, stop=True).then_inc(parts_summed, 1)
            pe.drain().then_inc(phase, 1)
            pe.wait_ge(phase, 5)
            pe.wait_ge(consts, 2)

            def gat_layer(n, L):
                w_hi, w_lo = ((w2_hi, w2_lo), (fc_hi, fc_lo))[n]
                width = (H, D)[n]
                pe.sem_inc(L.x_used, 1)

                by_node = (ps[3][:, 512:512 + HEADS], ps[0][:, 512:512 + HEADS])[n]

                def turn(t):
                    if t is None:
                        return
                    pe.wait_ge(L.gathered_ready, t.n + 1)
                    if not t.early(1):
                        pe.wait_ge(L.lo_ready, t.n)
                    for k in range(KH):
                        mm = pe.transpose(ps[1][:, k * P:(k + 1) * P], gathered[:, k * P:(k + 1) * P], ident[:])
                    mm.then_inc(L.turned, 1)

                def add(parts, one_hot, msgs, start=False, stop=False):
                    for i, msg in enumerate(msgs):
                        for half in range(2):
                            cols = slice(half * 512, half * 512 + 512)
                            pe.matmul(ps[2][:, cols], one_hot, msg[0:parts, cols], start=start and i == 0, stop=stop)

                def first_sums(t):
                    if t is None:
                        return
                    pe.wait_ge(L.msg_ready, t.n + 1)
                    add(C0, hot[:, t.s, :], (msg_hi[0], msg_lo[0]), start=True)
                    if n == 0:
                        add(C1, hot1[0:C1, t.s, :], (msg_hi[1],))

                def last_sums(t, after):
                    if t is None:
                        return
                    if n == 1 and not t.early(3):
                        pe.wait_ge(xT_ready, t.n - 2)
                    elif n == 0 and after is not None:
                        pe.wait_ge(L.e_ready, after.n + 1)
                    elif n == 0:
                        pe.wait_ge(L.extra_read, NT - 2)
                    pe.matmul(by_node, hot[:, t.s, :].bitcast(F32), weight[:, 0, :], start=True, stop=False)

                    def x_body(v, j):
                        pe.wait_ge(L.x_src_ready, v + 1)
                        pe.matmul(ps[3][:, 0:2 * HEADS], x_hot_t[:], x_maxima[:], start=True, stop=True).then_inc(L.x_at_edges, 1)
                        pe.wait_ge(L.x_msg_ready, v + 1)
                        add(P, x_hot[:], (x_msg,))
                        pe.matmul(by_node, x_hot[:], x_weight[:], start=False, stop=False).then_inc(L.x_used, 1)
                    more_chunks(pe, t, x_body)
                    if n == 0:
                        add(C1, hot1[0:C1, t.s, :], (msg_lo[1],), stop=True)
                    else:
                        pe.wait_ge(L.weighed, 2 * t.n + 2)
                        add(C1, hot1[0:C1, t.s, :].bitcast(F32), (msg_whole,), stop=True)
                    pe.matmul(by_node, hot1[0:C1, t.s, :].bitcast(F32), weight[0:C1, 1, :], start=False, stop=True).then_inc(L.summed, 1)

                def spread(t):
                    if t is None:
                        return
                    pe.wait_ge(L.diag_ready, t.n + 1)
                    if not t.early(1):
                        pe.wait_ge(L.e_ready, t.n)
                    if n == 0 and not t.early(2):
                        pe.wait_ge(L.denom_read, t.n - 1)
                    lag = (3, 5)[n]
                    if not t.early(lag):
                        pe.wait_ge(L.extra_read, t.n - lag + 1)
                    pe.matmul(ps[3][:, 0:512], ones[:], diag[0][:].rearrange("p h e -> p (h e)"), start=True, stop=True)
                    pe.matmul(ps[3][:, 640:640 + HEADS * C1], ones[0:C1, :], diag[1][0:C1, :, :].rearrange("p h e -> p (h e)"),
                              start=True, stop=True).then_inc(L.spread, 1)

                    def m_body(v, j):
                        pe.wait_ge(L.m_diag_ready, v + 1)
                        pe.matmul(ps[3][:, 0:512], ones[:], m_diag[:].rearrange("p h e -> p (h e)"), start=True, stop=True).then_inc(L.m_spread, 1)
                    more_chunks(pe, t, m_body)

                def at_edges(t):
                    if t is None:
                        return
                    pe.wait_ge(L.max_ready, t.n + 1)
                    for c in range(2):
                        mm = pe.matmul(ps[3][:, 520 + 8 * c:528 + 8 * c], hot_t[:, c * P:(c + 1) * P], maxima[:], start=True, stop=True)
                    mm.then_inc(L.at_edges, 1)

                def product(t, part, after, edges_of):
                    if t is None:
                        at_edges(edges_of)
                        return
                    if part == 0:
                        pe.wait_ge(L.lo_ready, t.n + 1)
                    if not t.early(1) and n == 0:
                        pe.wait_ge(L.copied, 2 * t.n - 1 + part)
                    elif not t.early(1) and part == 0:
                        pe.wait_ge(L.copied, t.n)
                    blocks = range(KH) if n == 0 else range(part * KH // 2, (part + 1) * KH // 2)
                    half = part if n == 0 else 0
                    cols = ps[0][:, half * 512:half * 512 + 512]
                    for k in blocks:
                        a = slice(k * P, (k + 1) * P)
                        w = slice(k * width + half * 512, k * width + half * 512 + 512)
                        if k == KH - 2:
                            at_edges(edges_of)
                        pe.matmul(cols, act_hi[:, a], w_hi[:, w], start=(k == 0), stop=False)
                        pe.matmul(cols, act_hi[:, a], w_lo[:, w], start=False, stop=False)
                        mm = pe.matmul(cols, act_lo[:, a], w_hi[:, w], start=False, stop=(k == KH - 1))
                    if n == 0 and part == 1:
                        pe.wait_ge(L.denom_read, after.n + 1 if after is not None else NT)
                        for k in range(KH):
                            a = slice(k * P, (k + 1) * P)
                            pe.matmul(ps[3][:, 536:552], act_hi[:, a], wa[1][:, k, :, :].rearrange("p v a -> p (v a)"), start=(k == 0), stop=False)
                            mm = pe.matmul(ps[3][:, 536:544], act_lo[:, a], wa_hi[1][:, k, :], start=False, stop=(k == KH - 1))
                    mm.then_inc((L.first_done, L.second_done)[part], 1)

                def gate_turn(t, after):
                    if t is None or n == 0:
                        return
                    pe.wait_ge(L.denom_read, after.n + 1 if after is not None else NT)
                    pe.wait_ge(xn2_ready, t.n + 1)
                    if not t.early(1):
                        pe.wait_ge(xT_ready, t.n)
                    for k in range(KD):
                        mm = pe.transpose(ps[0][:, 512 + k * P:512 + (k + 1) * P], result[:, t.s, D + k * P:D + (k + 1) * P], ident[:])
                    mm.then_inc(xn2_turned, 1)

                def gate_product(t, after):
                    if t is None or n == 0:
                        return
                    pe.wait_ge(xT_ready, t.n + 1)
                    pe.wait_ge(L.e_ready, after.n + 1 if after is not None else NT)
                    if not t.early(1):
                        pe.wait_ge(L.extra_read, t.n)
                    for k in range(KD):
                        mm = pe.matmul(ps[3][:, 544:552], xT[:, k * P:(k + 1) * P], gate_cols[:, k, :], start=(k == 0), stop=(k == KD - 1))
                    mm.then_inc(gates_done, 1)

                def step(s):
                    turn(s(0))
                    if n == 0:
                        first_sums(s(1))
                        spread(s(2))
                    else:
                        spread(s(2))
                        first_sums(s(1))
                    if n == 0:
                        product(s(0), 0, None, s(2))
                        last_sums(s(1), s(2))
                    else:
                        last_sums(s(1), None)
                        product(s(0), 0, None, None)
                        at_edges(s(2))
                    product(s(0), 1, s(1), None)
                    gate_product(s(-2), s(2))
                    gate_turn(s(-1), s(1))
                steps(pe, step, 2, 2)
                pe.drain().then_inc(phase, 1)
                pe.wait_ge(phase, 10 + 5 * n)
            gat_layer(0, layers[0])
            gat_layer(1, layers[1])
            for i in range(SINKHORN_ITERS):
                pe.wait_ge(share_ready, 3 * i + 1)
                pe.transpose(ps[3][0:EXPERTS, 0:P], col_a[:], ident[:]).then_inc(share_done, 1)
                pe.wait_ge(share_ready, 3 * i + 2)
                pe.matmul(ps[3][:, 512:520], ones[0:EXPERTS, :], col_diag[:], start=True, stop=True).then_inc(share_done, 1)
                pe.wait_ge(share_ready, 3 * i + 3)
                pe.matmul(ps[3][:, 520:528], ones[:], col_c[:], start=True, stop=True).then_inc(share_done, 1)
            with pe.Fori(0, FLOAT_BITS // BITS) as i:
                for b in range(BITS):
                    pe.wait_ge(share_ready, BITS * i + (b + 3 * SINKHORN_ITERS + 1))
                    pe.matmul(ps[3][:, 512:520], ones[:], col_a[:], start=True, stop=True).then_inc(share_done, 1)
            pe.wait_ge(share_ready, 3 * SINKHORN_ITERS + FLOAT_BITS + 1)
            for marks, within, whole in ((above_b, ps[0], ps[1]), (tie_b, ps[2], ps[3])):
                flat = marks[:].rearrange("p t e -> p (t e)")
                for a, b in ((0, 512), (512, NT * EXPERTS)):
                    pe.matmul(within[:, a:b], before_b[:], flat[:, a:b], start=True, stop=True)
                    mm = pe.matmul(whole[:, a:b], ones_b[:], flat[:, a:b], start=True, stop=True)
                mm.then_inc(share_done, 1)

            entries = ps[3][:, 0:EXPERTS * 3 * BLOCKS]
            width = 3 * BLOCKS

            def tile_entries(t):
                if t is None:
                    return
                pe.wait_ge(vals_ready, t.n + 1)
                if t.early(1):
                    pe.matmul(entries, zero_rb[:, 0:P], zero_rb[:], start=True, stop=False)
                for e in range(EXPERTS):
                    mm = pe.matmul(entries[:, e * width:(e + 1) * width], place_hot[:, t.s, e, :],
                                   block_val[:, t.s, e, :, :].rearrange("p v b -> p (v b)"), start=False, stop=False)
                mm.then_inc(hots_used, 1)

            def step(s):
                tile_entries(s(0))
            steps(pe, step, 0)
            pe.matmul(entries, zero_rb[:, 0:P], zero_rb[:], start=False, stop=True).then_inc(share_done, 1)
            pe.wait_ge(ew_hi_done, EXPERTS)
            pe.wait_ge(ew_lo_done, EXPERTS)

            def turn(t):
                if t is None:
                    return
                pe.wait_ge(tok_got[t.s], 16 * (t.h + 1))
                if not t.early(2):
                    pe.wait_ge(tok_lo, t.n - 1)
                for k in range(KD):
                    mm = pe.transpose(ps[1][:, t.s * 512 + k * P:t.s * 512 + (k + 1) * P], x_tok[:, t.s, k * P:(k + 1) * P], ident[:])
                mm.then_inc(tok_turned, 1)

            def product(t, expert):
                pe.wait_ge(tok_lo, t.n + 1)
                if not t.early(2):
                    pe.wait_ge(y_ready, t.n - 1)
                cols = ps[2 * t.s][:, 0:512]
                for k in range(KD):
                    a = slice(k * P, (k + 1) * P)
                    hi, lo = (w[:, bass.ds(expert, 1), k, :].rearrange("p o n -> p (o n)") for w in (ew_hi, ew_lo))
                    pe.matmul(cols, tT_hi[:, t.s, a], hi, start=(k == 0), stop=False)
                    pe.matmul(cols, tT_hi[:, t.s, a], lo, start=False, stop=False)
                    mm = pe.matmul(cols, tT_lo[:, t.s, a], hi, start=False, stop=(k == KD - 1))
                mm.then_inc(tok_done, 1)

            def expert_blocks(e):
                def at(b):
                    return Tile(e * (BLOCKS // 2) + b // 2, b % 2)
                for b in range(BLOCKS):
                    turn(at(b + 1) if not (isinstance(e, int) and at(b + 1).n == NB) else None)
                    product(at(b), e)
            turn(Tile(0, 0))
            expert_blocks(0)
            with pe.Fori(1, EXPERTS - 1) as e:
                expert_blocks(e)
            expert_blocks(EXPERTS - 1)

        @block.vector
        def _(dve):
            dve.wait_ge(edges_in, 64)
            dve.wait_ge(consts, 1)
            dve.tensor_tensor(e_other[:], e_src[:], e_dst[:], ALU.not_equal)
            dve.tensor_copy(e_row[:, :, 0], e_src[:])
            dve.tensor_copy(e_row[:].bitcast(F32)[:, :, 1], e_dst[:])
            dve.tensor_scalar(e_tmp[:], e_dst[:], 7, None, ALU.logical_shift_right)
            dve.drain()
            dve.tensor_copy(e_hi[:], e_tmp[:])
            dve.tensor_tensor_scan(e_count[:], e_other[:], zeros_e[:], 0.0, ALU.add, ALU.add)
            dve.tensor_scalar(e_self[:], e_other[:], -1.0, 1.0, ALU.mult, ALU.add)
            dve.drain()
            dve.tensor_scalar(e_tmp[:], e_dst[:], P - 1, None, ALU.bitwise_and)
            dve.tensor_copy(before_me[:], e_count[:, EC - 1:EC]).then_inc(parts_ready, 1)
            dve.drain()
            dve.tensor_copy(e_lo[:], e_tmp[:])
            dve.tensor_tensor(e_count[:], e_count[:], e_other[:], ALU.subtract)
            dve.drain()
            dve.scalar_tensor_tensor(e_count[:], e_self[:], float(NOWHERE), e_count[:], ALU.mult, ALU.add)
            dve.drain()
            dve.wait_ge(parts_summed, 1)
            dve.tensor_scalar(e_pos[:], e_count[:], ps[3][:, 512:513], None, ALU.add)
            dve.drain().then_inc(rows_ready, 1)

            for n in range(KD):
                dve.wait_ge(w_in[n % 2], 16 * (n // 2 + 1))
                dve.wait_ge(att_in[0], 32)
                for m in range(2):
                    dve.tensor_tensor(prod[:], stage[:, n % 2, :], att_vec[:, m, :], ALU.mult)
                    dve.drain()
                    dve.tensor_reduce(wa_f[0][:, n, m * HEADS:(m + 1) * HEADS], prod[:].rearrange("p (h c) -> p h c", h=HEADS), AX, ALU.add)
                    dve.drain()
                dve.wait_ge(w_hi_done, n + 1)
                dve.tensor_tensor(w1_lo[:, n * H:(n + 1) * H], stage[:, n % 2, :], w1_hi[:, n * H:(n + 1) * H].bitcast(F32), ALU.subtract)
                if n == KD - 1:
                    dve.tensor_copy(wa_hi[0], wa_f[0][:])
                    dve.drain()
                    dve.tensor_tensor(wa_lo[0], wa_f[0][:], wa_hi[0].bitcast(F32), ALU.subtract)
                dve.drain().then_inc(w_lo_done, 1)

            def statistics(t):
                if t is None:
                    return
                dve.wait_ge(x_got[t.s], 16 * (t.h + 1))
                dve.bn_stats(ln_stats[:, t.s, :], x_in[:, t.s, :])
                dve.drain()
                dve.bn_aggr(ln_mv[:, t.s, :], ln_stats[:, t.s, :]).then_inc(mv_ready, 1)

            def one_hots(t):
                if t is None:
                    return
                if not t.early(2):
                    dve.wait_ge(hot_used, t.n - 1)
                for u in range(2):
                    j, slot = bass.ds(2 * t.n + u, 1), 2 * t.s + u
                    dve.tensor_scalar(hot_lo[:, slot, :], iota[:], e_lo[:, j], None, ALU.is_equal)
                    dve.tensor_scalar(hot_hi[:, slot, 0:TT], iota[:, 0:TT], e_hi[:, j], e_self[:, j], ALU.is_equal, ALU.mult)
                    dve.tensor_scalar(hot_hi[:, slot, TT:2 * TT], iota[:, 0:TT], e_hi[:, j], e_other[:, j], ALU.is_equal, ALU.mult)
                dve.drain().then_inc(hot_ready, 1)

            def normalise(t):
                if t is None:
                    return
                dve.wait_ge(std_ready, t.n + 1)
                dve.reciprocal(ln_rstd[:, t.s, :], ln_std[:, t.s, :])
                dve.drain()
                dve.scalar_tensor_tensor(ln_step[:, t.s, :], ln_mv[:, t.s, 1:2], EPS_LN, ln_rstd[:, t.s, :], ALU.add, ALU.mult)
                dve.drain()
                dve.tensor_tensor(ln_step[:, t.s, :], ln_step[:, t.s, :], ln_rstd[:, t.s, :], ALU.mult)
                dve.drain()
                dve.tensor_scalar(ln_step[:, t.s, :], ln_step[:, t.s, :], -0.5, 1.5, ALU.mult, ALU.add)
                dve.drain()
                dve.tensor_tensor(ln_rstd[:, t.s, :], ln_rstd[:, t.s, :], ln_step[:, t.s, :], ALU.mult)
                dve.drain()
                if not t.early(2):
                    dve.wait_ge(xt_ready, t.n - 1)
                dve.tensor_scalar(x_norm[:, t.s, :], x_in[:, t.s, :], ln_mv[:, t.s, 0:1], ln_rstd[:, t.s, 0:1],
                                  ALU.subtract, ALU.mult).then_inc(xn_ready, 1)

            def low(t):
                if t is None:
                    return
                dve.wait_ge(xhi_ready, t.n + 1)
                dve.tensor_tensor(xT_lo[:, t.s, :], ps[1][:, t.s * 512:t.s * 512 + 512], xT_hi[:, t.s, :].bitcast(F32),
                                  ALU.subtract).then_inc(xlo_ready, 1)

            def right(t):
                if t is None:
                    return
                dve.wait_ge(h1_ready, t.n + 1)
                if not t.early(2):
                    dve.wait_ge(h1_stored[t.s], 16 * t.h)
                dve.tensor_copy(h_out[:, t.s, 512:H], ps[2 * t.s][:, 512:H])
                dve.tensor_reduce(att[0][:, bass.ds(t.n, 1), :].rearrange("p o a -> p (o a)"), ps[3][:, 512:528].rearrange("p (v a) -> p a v", v=2), AX, ALU.add)
                dve.drain().then_inc(h1_right, 1)

            def step(s):
                right(s(-1))
                one_hots(s(1))
                statistics(s(2))
                low(s(1))
                normalise(s(2))
            steps(dve, step, 2, 1)

            dve.wait_ge(counts_done, 1)
            dve.tensor_scalar(self_count[:], ps[3][:, 0:TT], 1.0, None, ALU.add)
            dve.tensor_copy(other_count[:], ps[3][:, TT:2 * TT])
            dve.drain().then_inc(parts_ready, 1)
            dve.wait_ge(parts_summed, 2)
            dve.tensor_copy(tile_sum[:], ps[3][:, 512:512 + TT])
            dve.drain()
            dve.tensor_tensor_scan(tile_scan[:], tile_sum[:], zeros_e[:, 0:TT], 0.0, ALU.add, ALU.add)
            dve.tensor_scalar(loops_i[:], tile_sum[0:1, :], float(P - 1 - C0 - C1), 0.0, ALU.add, ALU.max)
            dve.drain()
            dve.tensor_tensor(table[:, 0, :], tile_scan[0:1, :], tile_sum[0:1, :], ALU.subtract)
            dve.tensor_scalar(table[:, 1, :], loops_i[:], 7, None, ALU.logical_shift_right)
            dve.drain()
            dve.tensor_copy(loops_f[:], table[:, 1, :])
            dve.drain()
            dve.tensor_tensor_scan(loops_scan[:], loops_f[:], zeros_e[0:1, 0:TT], 0.0, ALU.add, ALU.add)
            dve.drain()
            dve.tensor_tensor(table[:, 2, :], loops_scan[:], loops_f[:], ALU.subtract)
            dve.drain().then_inc(table_done, 1)
            dve.drain().then_inc(phase, 1)
            dve.wait_ge(phase, 5)
            dve.wait_ge(small_in, 32)
            dve.wait_ge(consts, 2)

            def gat_layer(n, L):
                dve.sem_inc(L.m_used, 1)
                dve.wait_ge(bias_in, 16 * (n + 1))

                def low(t):
                    if t is None or n == 1:
                        return
                    dve.wait_ge(L.hi_ready, t.n + 1)
                    dve.scalar_tensor_tensor(act_lo[:], ps[1][:], 0.0, act_hi[:].bitcast(F32), ALU.max, ALU.subtract).then_inc(L.lo_ready, 1)

                def leaky(to, a):
                    dve.scalar_tensor_tensor(to, a, SLOPE, a, ALU.mult, ALU.max)

                def sources(t):
                    if t is None:
                        dve.drain()
                        return
                    dve.wait_ge(L.listed[t.s], 32 * (t.h + 1))
                    dve.tensor_scalar(at_tile[:, t.s, :], ix[:, t.s, :, :].bitcast(F32)[:, :, 1], tile_base[:, bass.ds(t.n, 1)], None, ALU.subtract)
                    dve.drain()
                    dve.tensor_scalar(off_tile[:, t.s, :], at_tile[:, t.s, :], float(P), float(NOWHERE), ALU.is_ge, ALU.mult)
                    dve.tensor_scalar(drop[:, t.s, :], at_tile[:, t.s, :], float(P), -BIG, ALU.is_ge, ALU.mult)
                    dve.drain()
                    dve.tensor_tensor(src_ok[:, t.s, :, :].rearrange("p c o -> p (c o)"), ix[:, t.s, :, 0], off_tile[:, t.s, :], ALU.add).then_inc(L.src_ready, 1)

                def keep_maxima(t):
                    if t is None:
                        return
                    dve.tensor_copy(x_maxima[:], maxima[:])

                def masks(t):
                    if t is None:
                        return
                    dve.tensor_scalar(hot[:, t.s, :], iota[:], at_tile[:, t.s, 0:1], None, ALU.is_equal)
                    dve.tensor_scalar(hot1[0:C1, t.s, :], iota[0:C1, :], at_tile[0:C1, t.s, 1:2], None, ALU.is_equal)
                    dve.tensor_scalar(hot_t[:, 0:C0 + C1], dst_row[:, t.s, :, :].bitcast(F32)[:, :, 1], node_id[:, bass.ds(t.n, 1)], None, ALU.is_equal)
                    dve.tensor_scalar(miss[:], dst_row[:, t.s, :, :].bitcast(F32)[:, :, 1], node_id[:, bass.ds(t.n, 1)], -BIG, ALU.not_equal, ALU.mult)
                    dve.drain()

                def highest(t, r):
                    if n == 0:
                        r = None
                    if t is None:
                        if r is not None:
                            dve.drain()
                            dve.bn_stats(ln2[:, 0:6], result[:, r.s, 0:D])
                            dve.drain()
                            dve.bn_aggr(ln2[:, 6:8], ln2[:, 0:6])
                            dve.drain()
                            dve.tensor_scalar(ln2[:, 8:9], ln2[:, 7:8], EPS_LN, None, ALU.add).then_inc(var_ready, 1)
                        return
                    dve.wait_ge(L.spread, t.n + 1)
                    for a, b, bank in ((0, C0, ps[3][:, 0:512]), (C0, C0 + C1, ps[3][:, 640:640 + HEADS * C1])):
                        dve.tensor_tensor(seen[:, :, a:b], bank.rearrange("p (h e) -> p h e", h=HEADS),
                                          miss[:, a:b].rearrange("p (o e) -> p o e", o=1).to_broadcast((P, HEADS, b - a)), ALU.add)
                    if r is not None:
                        dve.bn_stats(ln2[:, 0:6], result[:, r.s, 0:D])
                    dve.drain()
                    dve.tensor_reduce(top[:], seen[:], AX, ALU.max)
                    if r is not None:
                        dve.bn_aggr(ln2[:, 6:8], ln2[:, 0:6])
                    dve.drain()
                    mine = att[n][:, bass.ds(t.n, 1), :].rearrange("p o a -> p (o a)")
                    dve.tensor_tensor(top[:], top[:], mine[:, 0:HEADS], ALU.max)
                    if r is not None:
                        dve.tensor_scalar(ln2[:, 8:9], ln2[:, 7:8], EPS_LN, None, ALU.add).then_inc(var_ready, 1)
                    dve.drain()

                    def m_body(v, j):
                        dve.wait_ge(L.m_listed, 32 * (v + 1))
                        dve.tensor_scalar(m_small[:, 0:1], m_ix[:].bitcast(F32)[:, 1:2], tile_base[:, bass.ds(t.n, 1)], None, ALU.subtract)
                        dve.tensor_scalar(m_miss[:], m_row[:].bitcast(F32)[:, :, 1], node_id[:, bass.ds(t.n, 1)], None, ALU.is_equal)
                        dve.drain()
                        dve.tensor_scalar(m_small[:, 1:2], m_small[:, 0:1], float(P), float(NOWHERE), ALU.is_ge, ALU.mult)
                        dve.tensor_scalar(m_miss[:], m_miss[:], 1.0, BIG, ALU.subtract, ALU.mult)
                        dve.drain()
                        dve.tensor_tensor(m_src[:], m_ix[:, 0:1], m_small[:, 1:2], ALU.add).then_inc(L.m_src_ready, 1)
                        dve.wait_ge(L.m_spread, v + 1)
                        dve.tensor_tensor(seen[:, :, 0:P], ps[3][:, 0:512].rearrange("p (h e) -> p h e", h=HEADS),
                                          m_miss[:].rearrange("p (o e) -> p o e", o=1).to_broadcast((P, HEADS, P)), ALU.add)
                        dve.drain()
                        dve.tensor_reduce(m_top[:], seen[:, :, 0:P], AX, ALU.max)
                        dve.drain()
                        dve.tensor_tensor(top[:], top[:], m_top[:], ALU.max)
                        dve.drain().then_inc(L.m_used, 1)
                    more_chunks(dve, t, m_body)

                    dve.tensor_tensor(e_own[:, t.s, :], mine[:, 0:HEADS], mine[:, HEADS:2 * HEADS], ALU.add)
                    dve.tensor_tensor(top[:], top[:], mine[:, HEADS:2 * HEADS], ALU.add)
                    dve.tensor_copy(maxima[:, HEADS:2 * HEADS], mine[:, HEADS:2 * HEADS])
                    dve.drain()
                    leaky(maxima[:, 0:HEADS], top[:])
                    leaky(e_own[:, t.s, :], e_own[:, t.s, :])
                    dve.drain()
                    dve.tensor_tensor(e_own[:, t.s, :], e_own[:, t.s, :], maxima[:, 0:HEADS], ALU.subtract)
                    dve.drain().then_inc(L.max_ready, 1)

                def low_messages(t, c):
                    if t is None:
                        return
                    rows = (C0, C1)[c]
                    dve.wait_ge(L.weighed, 2 * t.n + 1 + c)
                    for m in range(HEADS):
                        cols = slice(m * HID, (m + 1) * HID)
                        mm = dve.scalar_tensor_tensor(msg_lo[c][0:rows, cols], near_h[c][0:rows, t.s, cols], weight[0:rows, c, m:m + 1],
                                                      msg_hi[c][0:rows, cols].bitcast(F32), ALU.mult, ALU.subtract)
                    if c == 1 - n:
                        dve.drain().then_inc(L.msg_ready, 1)

                def x_body_of(t):
                    def x_body(v, j):
                        dve.wait_ge(L.x_listed, 32 * (v + 1))
                        dve.tensor_scalar(x_small[:, 0:1], x_ix[:].bitcast(F32)[:, 1:2], tile_base[:, bass.ds(t.n, 1)], None, ALU.subtract)
                        dve.tensor_scalar(x_hot_t[:], x_row[:].bitcast(F32)[:, :, 1], node_id[:, bass.ds(t.n, 1)], None, ALU.is_equal)
                        dve.drain()
                        dve.tensor_scalar(x_hot[:], iota[:], x_small[:, 0:1], None, ALU.is_equal)
                        dve.tensor_scalar(x_small[:, 1:2], x_small[:, 0:1], float(P), float(NOWHERE), ALU.is_ge, ALU.mult)
                        dve.tensor_scalar(x_small[:, 2:3], x_small[:, 0:1], float(P), -BIG, ALU.is_ge, ALU.mult)
                        dve.drain()
                        dve.tensor_tensor(x_src[:], x_ix[:, 0:1], x_small[:, 1:2], ALU.add)
                        dve.drain().then_inc(L.x_src_ready, 1)
                        dve.wait_ge(L.x_at_edges, v + 1)
                        dve.wait_ge(L.x_got, 32 * (v + 1))
                        dve.tensor_tensor(x_e[:], x_att[:, 0:HEADS], ps[3][:, HEADS:2 * HEADS], ALU.add)
                        dve.drain()
                        leaky(x_e[:], x_e[:])
                        dve.drain()
                        dve.tensor_tensor(x_e[:], x_e[:], ps[3][:, 0:HEADS], ALU.subtract).then_inc(L.x_e_ready, 1)
                    return x_body

                def denominators(t):
                    if t is None:
                        return
                    dve.wait_ge(L.summed, t.n + 1)
                    dve.scalar_tensor_tensor(denom[:], (ps[3], ps[0])[n][:, 512:512 + HEADS], 1e-16, weight_own[:, t.s, :], ALU.add, ALU.add).then_inc(L.denom_read, 1)

                def gather(t):
                    if t is None:
                        return
                    dve.wait_ge(L.own_ready, t.n + 1)
                    dve.tensor_tensor(own_msg[:], ps[2][:], own_msg[:], ALU.add)
                    dve.drain()
                    dve.reciprocal(denom[:], denom[:])
                    dve.drain()
                    if not t.early(1):
                        dve.wait_ge(L.turned if n == 0 else L.lo_ready, t.n)
                    for m in range(HEADS):
                        c = slice(m * HID, (m + 1) * HID)
                        dve.scalar_tensor_tensor(gathered[:, c], own_msg[:, c], denom[:, m:m + 1], bias_row[:, c], ALU.mult, ALU.add)
                    dve.drain().then_inc(L.gathered_ready, 1)

                def terms(t):
                    if t is None or n == 1:
                        return
                    dve.wait_ge(L.second_done, t.n + 1)
                    dve.tensor_reduce(att[1][:, bass.ds(t.n, 1), :].rearrange("p o a -> p (o a)"), ps[3][:, 536:552].rearrange("p (v a) -> p a v", v=2), AX, ALU.add).then_inc(L.extra_read, 1)

                def gate_terms(t):
                    if t is None or n == 0:
                        return
                    dve.wait_ge(gates_done, t.n + 1)
                    dve.tensor_copy(gates[:, bass.ds(t.n, 1), :].rearrange("p o a -> p (o a)"), ps[3][:, 544:552]).then_inc(L.extra_read, 1)

                def residual(t):
                    if t is None or n == 0:
                        return
                    if t.early(2):
                        dve.wait_ge(L.second_done, t.n + 1)
                    else:
                        dve.wait_ge(L.stored[t.s], 32 * t.h)
                    dve.wait_ge(x_plus_ready, t.n + 1)
                    dve.tensor_tensor(result[:, t.s, 0:D], ps[0][:, 0:D], x_plus[:], ALU.add).then_inc(L.copied, 1)

                def exponents(t, r):
                    if t is not None:
                        dve.wait_ge(L.at_edges, t.n + 1)
                        at = ps[3][:, 520:536].rearrange("p (c a) -> p c a", c=2)
                        dve.tensor_tensor(e_in[:], near_att[:, t.s, :, 0:HEADS], at[:, :, HEADS:2 * HEADS], ALU.add)
                        dve.drain()
                        leaky(e_in[:], e_in[:])
                        dve.drain()
                        dve.tensor_tensor(e_in[:], e_in[:], at[:, :, 0:HEADS], ALU.subtract).then_inc(L.e_ready, 1)
                    if r is None:
                        return
                    dve.wait_ge(pow_ready, r.n + 1)
                    dve.tensor_tensor(ln2[:, 10:11], ln2[:, 9:10], ln2[:, 9:10], ALU.mult)
                    dve.drain()
                    dve.tensor_tensor(ln2[:, 10:11], ln2[:, 10:11], ln2[:, 8:9], ALU.mult)
                    dve.drain()
                    dve.tensor_scalar(ln2[:, 10:11], ln2[:, 10:11], -0.5, 1.5, ALU.mult, ALU.add)
                    dve.drain()
                    dve.tensor_tensor(ln_scale[:, r.s, 0:1], ln2[:, 9:10], ln2[:, 10:11], ALU.mult)
                    dve.drain()
                    dve.scalar_tensor_tensor(ln_scale[:, r.s, 1:2], ln2[:, 6:7], -1.0, ln_scale[:, r.s, 0:1], ALU.mult, ALU.mult).then_inc(scale_ready, 1)

                def step(s):
                    terms(s(-1))
                    residual(s(-1))
                    keep_maxima(s(1))
                    sources(s(3))
                    low(s(0))
                    highest(s(2), s(-1))
                    if n == 0:
                        exponents(s(2), None)
                    if s(1) is not None:
                        more_chunks(dve, s(1), x_body_of(s(1)))
                    if n == 1:
                        exponents(s(2), s(-1))
                    denominators(s(1))
                    gather(s(1))
                    gate_terms(s(-2))
                    masks(s(3))
                    low_messages(s(2), 0)
                    if n == 0:
                        low_messages(s(2), 1)
                steps(dve, step, 3, 3)
                dve.drain().then_inc(phase, 1)
                dve.wait_ge(phase, 10 + 5 * n)
            gat_layer(0, layers[0])
            gat_layer(1, layers[1])
            dve.wait_ge(consts, 3)
            dve.tensor_scalar(work[:], gates[:], GATE_MIN, None, ALU.max)
            dve.drain().then_inc(to_log, 1)
            dve.wait_ge(from_log, 1)

            def by_token(a):
                return a.rearrange("p (t o) -> p t o", o=1).to_broadcast((P, NT, EXPERTS))

            def by_expert(a):
                return a.rearrange("p (o e) -> p o e", o=1).to_broadcast((P, NT, EXPERTS))

            def mask_outside():
                dve.drain()
                dve.tensor_scalar(logp[:, NT - 1, :], logp[:, NT - 1, :], outside_neg[:, 0:1], None, ALU.add)
                dve.drain()

            mask_outside()
            for i in range(SINKHORN_ITERS):
                dve.tensor_reduce(col_a[:], logp[:].rearrange("p t e -> p e t"), AX, ALU.max).then_inc(share_ready, 1)
                dve.wait_ge(share_done, 3 * i + 1)
                dve.tensor_reduce(col_t[:], ps[3][0:EXPERTS, 0:P], AX, ALU.max)
                dve.drain()
                dve.tensor_scalar(col_diag[:], ident[0:EXPERTS, 0:EXPERTS], col_t[:, 0:1], None, ALU.mult).then_inc(share_ready, 1)
                dve.wait_ge(share_done, 3 * i + 2)
                dve.tensor_copy(col_a[:], ps[3][:, 512:520])
                dve.drain()
                dve.tensor_tensor(work[:], logp[:], by_expert(col_a[:]), ALU.subtract).then_inc(to_log, 1)
                dve.wait_ge(from_log, 4 * i + 2)
                dve.tensor_reduce(col_c[:], work[:].rearrange("p t e -> p e t"), AX, ALU.add).then_inc(share_ready, 1)
                dve.wait_ge(from_log, 4 * i + 3)
                dve.tensor_tensor(col_a[:], col_a[:], col_b[:], ALU.add)
                dve.drain()
                dve.tensor_tensor(logp[:], logp[:], by_expert(col_a[:]), ALU.subtract)
                dve.drain()
                dve.tensor_reduce(row_a[:], logp[:], AX, ALU.max)
                dve.drain()
                dve.tensor_tensor(work[:], logp[:], by_token(row_a[:]), ALU.subtract).then_inc(to_log, 1)
                dve.wait_ge(from_log, 4 * i + 4)
                dve.tensor_reduce(row_b[:], work[:], AX, ALU.add).then_inc(to_log, 1)
                dve.wait_ge(from_log, 4 * i + 5)
                dve.tensor_tensor(row_a[:], row_a[:], row_b[:], ALU.add)
                dve.drain()
                dve.tensor_tensor(logp[:], logp[:], by_token(row_a[:]), ALU.subtract)
                if i < SINKHORN_ITERS - 1:
                    mask_outside()
            dve.drain().then_inc(to_log, 1)
            dve.wait_ge(from_log, 4 * SINKHORN_ITERS + 2)
            dve.tensor_scalar(prob[:, NT - 1, :], prob[:, NT - 1, :], inside[:, 0:1], outside[:, NT - 1:NT], ALU.mult, ALU.subtract)
            dve.drain()

            with dve.Fori(0, FLOAT_BITS // BITS) as i:
                for b in range(BITS):
                    dve.tensor_tensor(trial[:], found[:], bit[:], ALU.bitwise_or)
                    dve.drain()
                    dve.tensor_tensor(work[:], prob[:], by_expert(trial[:].bitcast(F32)), ALU.is_ge)
                    dve.drain()
                    dve.tensor_reduce(col_a[:], work[:].rearrange("p t e -> p e t"), AX, ALU.add).then_inc(share_ready, 1)
                    dve.wait_ge(share_done, BITS * i + (b + 3 * SINKHORN_ITERS + 1))
                    dve.scalar_tensor_tensor(trial[:], ps[3][:, 512:520], float(TOPK), bit[:], ALU.is_ge, ALU.mult)
                    dve.drain()
                    dve.tensor_tensor(found[:], found[:], trial[:], ALU.bitwise_or)
                    dve.tensor_scalar(bit[:], bit[:], 1, None, ALU.logical_shift_right)
                    dve.drain()

            dve.tensor_tensor(above[:], prob[:], by_expert(found[:].bitcast(F32)), ALU.is_gt)
            dve.tensor_tensor(tie[:], prob[:], by_expert(found[:].bitcast(F32)), ALU.is_equal)
            dve.drain()
            dve.tensor_copy(above_b[:], above[:])
            dve.tensor_copy(tie_b[:], tie[:])
            dve.drain().then_inc(share_ready, 1)

            def ranks(within, whole):
                dve.tensor_copy(work[:].rearrange("p t e -> p (t e)"), whole[:, 0:NT * EXPERTS])
                dve.drain()
                for e in range(EXPERTS):
                    dve.tensor_tensor_scan(scan[:, :, e], work[:, :, e], zeros_r[:], 0.0, ALU.add, ALU.add)
                dve.drain()
                dve.tensor_tensor(work[:], scan[:], work[:], ALU.subtract)
                dve.tensor_copy(col_a[:], scan[:, NT - 1, :])
                dve.drain()
                dve.tensor_tensor(place[:].rearrange("p t e -> p (t e)"), within[:, 0:NT * EXPERTS], work[:].rearrange("p t e -> p (t e)"), ALU.add)
                dve.drain()

            dve.wait_ge(share_done, 3 * SINKHORN_ITERS + FLOAT_BITS + 2)
            ranks(ps[0], ps[1])
            dve.tensor_copy(col_b[:], col_a[:])
            dve.tensor_tensor(place_hi[:], place[:], above[:], ALU.mult)
            dve.drain()
            ranks(ps[2], ps[3])
            dve.tensor_scalar(col_c[:], col_b[:], -1.0, float(TOPK), ALU.mult, ALU.add)
            dve.drain()
            dve.tensor_tensor(work[:], place[:], by_expert(col_c[:]), ALU.is_lt)
            dve.tensor_tensor(place[:], place[:], by_expert(col_b[:]), ALU.add)
            dve.drain()
            dve.tensor_tensor(tie[:], tie[:], work[:], ALU.mult)
            dve.drain()
            dve.tensor_tensor(place[:], place[:], tie[:], ALU.mult)
            dve.tensor_tensor(above[:], above[:], tie[:], ALU.add)
            dve.drain()
            dve.tensor_tensor(place[:], place[:], place_hi[:], ALU.add)
            dve.tensor_scalar(work[:], above[:], -float(NOWHERE), float(NOWHERE), ALU.mult, ALU.add)
            dve.tensor_reduce(row_a[:], above[:], AX, ALU.add)
            dve.scalar_tensor_tensor(code[:], prob[:], 0.5, above[:], ALU.is_gt, ALU.mult)
            dve.drain()
            dve.tensor_tensor(place_i[:], place[:], work[:], ALU.add)
            dve.tensor_scalar(row_a[:], row_a[:], 1.0, None, ALU.add)
            dve.drain()
            dve.tensor_scalar(work[:].bitcast(I32), place_i[:], 7, None, ALU.logical_shift_right)
            dve.tensor_scalar(scan[:].bitcast(I32), place_i[:], P - 1, None, ALU.bitwise_and)
            dve.tensor_tensor(code[:], code[:], by_token(row_a[:]), ALU.mult)
            dve.drain()
            dve.tensor_copy(place_hi[:], work[:].bitcast(I32))
            dve.tensor_copy(place_lo[:], scan[:].bitcast(I32))
            dve.drain()

            def hots(t):
                if t is None:
                    return
                if not t.early(2):
                    dve.wait_ge(hots_used, t.n - 1)
                lo = place_lo[:, bass.ds(t.n, 1), :].rearrange("p o e -> p (e o)")
                hi = place_hi[:, bass.ds(t.n, 1), :].rearrange("p o e -> p (e o)")

                def wide(a, n):
                    return a.rearrange("p (e o) -> p e o", o=1).to_broadcast((P, EXPERTS, n))
                dve.tensor_tensor(place_hot[:, t.s, :, :], iota_b[:].rearrange("p (o n) -> p o n", o=1).to_broadcast((P, EXPERTS, P)), wide(lo, P), ALU.is_equal)
                dve.tensor_tensor(block_hot[:, t.s, :, :], iota[:, 0:BLOCKS].rearrange("p (o n) -> p o n", o=1).to_broadcast((P, EXPERTS, BLOCKS)), wide(hi, BLOCKS), ALU.is_equal)
                dve.drain().then_inc(hots_ready, 1)

            def step(s):
                hots(s(0))
            steps(dve, step, 0)
            dve.wait_ge(share_done, 3 * SINKHORN_ITERS + FLOAT_BITS + 3)
            dve.tensor_copy(listed_f[:].rearrange("p e v b -> p (e v b)"), ps[3][:, 0:EXPERTS * 3 * BLOCKS])
            dve.drain()
            dve.scalar_tensor_tensor(token_f[:], listed_f[:, :, 0, :], float(P), listed_f[:, :, 1, :], ALU.mult, ALU.add)
            dve.tensor_scalar(place[:, 0:BLOCKS, :].rearrange("p b e -> p e b"), listed_f[:, :, 2, :], 1.0, None, ALU.max)
            dve.drain()
            dve.scalar_tensor_tensor(token_f[:, :, BLOCKS - 1], token_f[:, :, 0], past_end[:, 0:1], token_f[:, :, BLOCKS - 1], ALU.mult, ALU.add)
            dve.reciprocal(scan[:, 0:BLOCKS, :].rearrange("p b e -> p e b"), place[:, 0:BLOCKS, :].rearrange("p b e -> p e b"))
            dve.drain()
            dve.tensor_copy(token[:].rearrange("p (e b) o -> p e (b o)", e=EXPERTS), token_f[:])
            dve.scalar_tensor_tensor(factor[:].rearrange("p (e b) o -> p e (b o)", e=EXPERTS), listed_f[:, :, 2, :], 0.0,
                                     scan[:, 0:BLOCKS, :].rearrange("p b e -> p e b"), ALU.is_gt, ALU.mult)
            dve.drain().then_inc(lists_ready, 1)

            def fetch_index(t):
                if t is None:
                    return
                if not t.early(2):
                    dve.wait_ge(tok_got[t.s], 16 * t.h)
                dve.tensor_copy(fetch_at[:, t.s, :], token[:, bass.ds(t.n, 1), :].rearrange("p o w -> p (o w)")).then_inc(fetch_ready, 1)

            def add_index(t):
                if t is None:
                    return
                if not t.early(2):
                    dve.wait_ge(added, 16 * (t.n - 1))
                dve.tensor_copy(add_at[:, t.s, :], token[:, bass.ds(t.n, 1), :].rearrange("p o w -> p (o w)")).then_inc(add_ready, 1)

            def low(t):
                if t is None:
                    return
                dve.wait_ge(tok_hi, t.n + 1)
                dve.tensor_tensor(tT_lo[:, t.s, :], ps[1][:, t.s * 512:t.s * 512 + 512], tT_hi[:, t.s, :].bitcast(F32), ALU.subtract).then_inc(tok_lo, 1)

            def step(s):
                fetch_index(s(3))
                low(s(1))
                add_index(s(0))
            steps(dve, step, 3, 0, NB)


_INS = ['x', 'src', 'dst', 'L0_gnn_W1', 'L0_gnn_att_src1', 'L0_gnn_att_dst1', 'L0_gnn_b1', 'L0_gnn_W2', 'L0_gnn_att_src2',
        'L0_gnn_att_dst2', 'L0_gnn_b2', 'L0_gnn_fcW', 'L0_gnn_fcb', 'L0_ffn_gate_w', 'L0_ffn_experts']
_OUTS = [((N, D), 'float32')]


def kernel(**inputs):
    import numpy as _np
    import concourse.bacc as _bacc
    from concourse import mybir as _mybir
    from concourse.bass_utils import run_bass_kernel_spmd as _run

    nc = _bacc.Bacc("TRN2", target_bir_lowering=False, num_devices=1)
    arrays, args = {}, []
    for name in _INS:
        a = _np.ascontiguousarray(inputs[name])
        arrays[f"in_{name}_dram"] = a
        args.append(nc.dram_tensor(f"in_{name}_dram", a.shape, _mybir.dt.from_np(a.dtype), kind="ExternalInput").ap())
    for i, (shape, dtype) in enumerate(_OUTS):
        dt = _mybir.dt.from_np(_np.dtype(dtype))
        args.append(nc.dram_tensor(f"out_{i}_dram", shape, dt, kind="ExternalOutput").ap())
    gnn_ffn_kernel(nc, *args)
    r = _run(nc, [arrays], core_ids=[0])
    got = tuple(r.results[0][f"out_{i}_dram"] for i in range(len(_OUTS)))
    return got[0]
```
